# Optimizing a Trainium2 kernel written in Bass

```python
import numpy as np
import jax
import jax.numpy as jnp

def _softmax(x, axis=-1):
    return jax.nn.softmax(x, axis=axis)

def _gelu(x):
    return jax.nn.gelu(x, approximate=True)

def _silu(x):
    return jax.nn.silu(x)

def _sigmoid(x):
    return jax.nn.sigmoid(x)

def _layernorm(x, axis=-1, eps=1e-05):
    m = jnp.mean(x, axis=axis, keepdims=True)
    v = jnp.var(x, axis=axis, keepdims=True)
    return (x - m) / jnp.sqrt(v + eps)

def _scatter_add(tgt, idx, src, axis=0):
    return tgt.at[idx].add(src)

def _segment_sum(src, seg, n):
    return jax.ops.segment_sum(src, seg, n)
kernel_name = 'mk_seq_preln_d1_jaxref_r8_88239e'

def setup_inputs(seed: int=0):
    np.random.seed(seed)
    _w = jnp.asarray

    def _L0_attn_setup():
        import jax, jax.numpy as jnp
        import numpy as np
        INDIM = 128
        NHEADS = 16
        DK = INDIM // NHEADS
        DV = INDIM // NHEADS
        B, S = (4, 256)
        key = jax.random.key(seed)
        ks = jax.random.split(key, 5)
        x = jax.random.normal(ks[0], (B, S, INDIM), dtype=jnp.float32)
        std_qk = np.sqrt(2.0 / (INDIM + DK)).astype(np.float32)
        std_v = np.sqrt(2.0 / (INDIM + DV)).astype(np.float32)
        Wq = jax.random.normal(ks[1], (NHEADS * DK, INDIM), dtype=jnp.float32) * std_qk
        Wk = jax.random.normal(ks[2], (NHEADS * DK, INDIM), dtype=jnp.float32) * std_qk
        Wv = jax.random.normal(ks[3], (NHEADS * DV, INDIM), dtype=jnp.float32) * std_v
        std_o = np.sqrt(2.0 / (NHEADS * DV + INDIM)).astype(np.float32)
        Wo = jax.random.normal(ks[4], (INDIM, NHEADS * DV), dtype=jnp.float32) * std_o
        bq = jnp.zeros((NHEADS * DK,), jnp.float32)
        bk = jnp.zeros((NHEADS * DK,), jnp.float32)
        bv = jnp.zeros((NHEADS * DV,), jnp.float32)
        bo = jnp.zeros((INDIM,), jnp.float32)
        return {'x': x, 'Wq': Wq, 'bq': bq, 'Wk': Wk, 'bk': bk, 'Wv': Wv, 'bv': bv, 'Wo': Wo, 'bo': bo}
    _L0_attn_in = _L0_attn_setup()

    def _L0_ffn_setup():
        import jax, jax.numpy as jnp
        import numpy as np
        NUM_NOD = 6
        MAX_PREV = 5
        NUM_EDGE = 20
        D = 128
        H = 8
        LN_EPS = 1e-06

        def _layernorm(x, g, b):
            mu = jnp.mean(x, axis=-1, keepdims=True)
            var = jnp.mean(jnp.square(x - mu), axis=-1, keepdims=True)
            return (x - mu) * jax.lax.rsqrt(var + LN_EPS) * g + b

        def _mha(q, k, v, wq, wk, wv, wo):
            B, S, d = q.shape
            dh = d // H
            qh = (q @ wq).reshape(B, S, H, dh)
            kh = (k @ wk).reshape(B, S, H, dh)
            vh = (v @ wv).reshape(B, S, H, dh)
            scores = jnp.einsum('bqhd,bkhd->bhqk', qh, kh) / jnp.sqrt(jnp.asarray(dh, q.dtype))
            attn = jax.nn.softmax(scores, axis=-1)
            ctx = jnp.einsum('bhqk,bkhd->bqhd', attn, vh).reshape(B, S, d)
            return ctx @ wo
        key = jax.random.key(seed)
        ks = jax.random.split(key, 12)
        B, S = (8, 128)
        scale = 1.0 / np.sqrt(D)
        return {'inputs': jax.random.normal(ks[0], (B, S, D), jnp.float32), 'ew': jax.random.uniform(ks[1], (NUM_NOD, 3), jnp.float32), 'act_w': jax.random.uniform(ks[2], (NUM_NOD,), jnp.float32), 'We': jax.random.normal(ks[3], (NUM_EDGE, D, D), jnp.float32) * scale, 'be': jnp.zeros((NUM_EDGE, D), jnp.float32), 'Wq': jax.random.normal(ks[4], (NUM_NOD, D, D), jnp.float32) * scale, 'Wk': jax.random.normal(ks[5], (NUM_NOD, D, D), jnp.float32) * scale, 'Wv': jax.random.normal(ks[6], (NUM_NOD, D, D), jnp.float32) * scale, 'Wo': jax.random.normal(ks[7], (NUM_NOD, D, D), jnp.float32) * scale, 'ln_g': jnp.ones((D,), jnp.float32), 'ln_b': jnp.zeros((D,), jnp.float32)}
    _L0_ffn_in = _L0_ffn_setup()
    _d = {'L0_attn_x': _L0_attn_in['x'], 'L0_attn_Wq': _L0_attn_in['Wq'], 'L0_attn_bq': _L0_attn_in['bq'], 'L0_attn_Wk': _L0_attn_in['Wk'], 'L0_attn_bk': _L0_attn_in['bk'], 'L0_attn_Wv': _L0_attn_in['Wv'], 'L0_attn_bv': _L0_attn_in['bv'], 'L0_attn_Wo': _L0_attn_in['Wo'], 'L0_attn_bo': _L0_attn_in['bo'], 'L0_ffn_ew': _L0_ffn_in['ew'], 'L0_ffn_act_w': _L0_ffn_in['act_w'], 'L0_ffn_We': _L0_ffn_in['We'], 'L0_ffn_be': _L0_ffn_in['be'], 'L0_ffn_Wq': _L0_ffn_in['Wq'], 'L0_ffn_Wk': _L0_ffn_in['Wk'], 'L0_ffn_Wv': _L0_ffn_in['Wv'], 'L0_ffn_Wo': _L0_ffn_in['Wo'], 'L0_ffn_ln_g': _L0_ffn_in['ln_g'], 'L0_ffn_ln_b': _L0_ffn_in['ln_b']}
    _x0 = _d['L0_attn_x']
    _d['L0_attn_x'] = jax.random.normal(jax.random.fold_in(jax.random.key(seed), 1), (4, 1024, 128), dtype=_x0.dtype)
    del _x0
    return _d

def reference(L0_attn_x, L0_attn_Wq, L0_attn_bq, L0_attn_Wk, L0_attn_bk, L0_attn_Wv, L0_attn_bv, L0_attn_Wo, L0_attn_bo, L0_ffn_ew, L0_ffn_act_w, L0_ffn_We, L0_ffn_be, L0_ffn_Wq, L0_ffn_Wk, L0_ffn_Wv, L0_ffn_Wo, L0_ffn_ln_g, L0_ffn_ln_b):

    def _L0_attn_ref(x, Wq, bq, Wk, bk, Wv, bv, Wo, bo):
        import jax, jax.numpy as jnp
        import numpy as np
        INDIM = 128
        NHEADS = 16
        DK = INDIM // NHEADS
        DV = INDIM // NHEADS
        B, S = (4, 256)
        b, s, _ = x.shape
        q = (x @ Wq.T + bq).reshape(b, s, NHEADS, DK)
        k = (x @ Wk.T + bk).reshape(b, s, NHEADS, DK)
        v = (x @ Wv.T + bv).reshape(b, s, NHEADS, DV)
        w = jnp.einsum('bshd,bzhd->bhsz', q, k)
        w = w / jnp.sqrt(jnp.float32(DV))
        w = jax.nn.softmax(w, axis=-1)
        vw = jnp.einsum('bhsz,bzhd->bshd', w, v)
        vw = vw.reshape(b, s, NHEADS * DV)
        out = vw @ Wo.T + bo
        return out

    def _L0_ffn_ref(inputs, ew, act_w, We, be, Wq, Wk, Wv, Wo, ln_g, ln_b):
        import jax, jax.numpy as jnp
        import numpy as np
        NUM_NOD = 6
        MAX_PREV = 5
        NUM_EDGE = 20
        D = 128
        H = 8
        LN_EPS = 1e-06

        def _layernorm(x, g, b):
            mu = jnp.mean(x, axis=-1, keepdims=True)
            var = jnp.mean(jnp.square(x - mu), axis=-1, keepdims=True)
            return (x - mu) * jax.lax.rsqrt(var + LN_EPS) * g + b

        def _mha(q, k, v, wq, wk, wv, wo):
            B, S, d = q.shape
            dh = d // H
            qh = (q @ wq).reshape(B, S, H, dh)
            kh = (k @ wk).reshape(B, S, H, dh)
            vh = (v @ wv).reshape(B, S, H, dh)
            scores = jnp.einsum('bqhd,bkhd->bhqk', qh, kh) / jnp.sqrt(jnp.asarray(dh, q.dtype))
            attn = jax.nn.softmax(scores, axis=-1)
            ctx = jnp.einsum('bhqk,bkhd->bqhd', attn, vh).reshape(B, S, d)
            return ctx @ wo
        nodes = {-1: inputs}
        lind = 0
        for c in range(NUM_NOD):
            nsrc = min(c + 1, MAX_PREV)
            snode = c - nsrc
            eq, ek, ev = (lind + nsrc - 1, lind, lind + nsrc // 2)
            in_q, in_k, in_v = (c - 1, snode, snode + nsrc // 2)
            q = ew[c, 0] * (nodes[in_q] @ We[eq] + be[eq])
            k = ew[c, 1] * (nodes[in_k] @ We[ek] + be[ek])
            v = ew[c, 2] * (nodes[in_v] @ We[ev] + be[ev])
            o = _mha(q, k, v, Wq[c], Wk[c], Wv[c], Wo[c])
            nodes[c] = act_w[c] * o + q
            lind += nsrc
        out = nodes[NUM_NOD - 1]
        return _layernorm(out, ln_g, ln_b)
    x = L0_attn_x
    x = x + _L0_attn_ref(_layernorm(x, axis=-1), L0_attn_Wq, L0_attn_bq, L0_attn_Wk, L0_attn_bk, L0_attn_Wv, L0_attn_bv, L0_attn_Wo, L0_attn_bo)
    x = x + _L0_ffn_ref(_layernorm(x, axis=-1), L0_ffn_ew, L0_ffn_act_w, L0_ffn_We, L0_ffn_be, L0_ffn_Wq, L0_ffn_Wk, L0_ffn_Wv, L0_ffn_Wo, L0_ffn_ln_g, L0_ffn_ln_b)
    return x

_drawn_inputs = setup_inputs


def setup_inputs(seed=0):
    import zlib

    import numpy as np

    out = dict(_drawn_inputs(seed))
    spreads = {'L0_attn_bq': (0.0, 0.439),
     'L0_attn_bk': (0.0, 2.0),
     'L0_attn_bv': (0.0, 0.1),
     'L0_attn_bo': (0.0, 0.1),
     'L0_ffn_be': (0.0, 0.1),
     'L0_ffn_ln_g': (1.0, 0.2),
     'L0_ffn_ln_b': (0.0, 0.1)}
    factors = {'L0_ffn_Wq': 64.0, 'L0_ffn_Wk': 64.0}
    for name, (base, spread) in spreads.items():
        noise = np.random.default_rng([zlib.crc32(name.encode()), seed]).standard_normal(out[name].shape)
        drawn = base * np.exp(spread * noise) if base else spread * noise
        out[name] = jnp.asarray(drawn.astype(out[name].dtype))
    for name, factor in factors.items():
        out[name] = (out[name] * factor).astype(out[name].dtype)
    return out
```

```python
from contextlib import ExitStack

import concourse.bass as bass
from concourse import mybir

F32 = mybir.dt.float32
BF16 = mybir.dt.bfloat16
ALU = mybir.AluOpType
ACT = mybir.ActivationFunctionType
AX = mybir.AxisListType

D = 128
B = 4
S = 1024
NODES = 6
MAX_PREV = 5
HEADS = 8
DH = 16
TERMS = 6
KR = TERMS * DH
KM = KR + 3
GROUP = 4
NB = S // 128
ATTN_STEPS = 2 * B
STEPS = ATTN_STEPS + NODES * B
SLOTS = 32
PRING = 4

AT_MROW1, AT_K, AT_Q1, AT_Q, AT_V, AT_OUT, AT_T1, AT_MROW0, AT_T2 = 1, 2, 4, 6, 11, 14, 17, 19, 29
AT_DEN, AT_RDEN = 2, 8


def has_b(g):
    return 0 <= g < STEPS


def has_max(g):
    return 0 <= g + 1 < STEPS


def has_proj(g):
    return 0 <= g + 2 < STEPS


def has_out(g):
    return 0 <= g - 1 < STEPS


def tail(g):
    s = g - 1
    if 0 <= s < ATTN_STEPS:
        return "mid" if s % 2 else ""
    return "last" if STEPS - B <= s < STEPS else ""


def ring_uses(g):
    uses = []
    for n in range(SLOTS):
        uses += chores(g, n)
        if has_max(g):
            uses += [("max", 2 * n), ("max", 2 * n + 1)]
    return uses


def chores(g, n):
    out = []
    if n == AT_MROW1 and has_b(g):
        out.append(("mrow", 1))
    if n == AT_K and has_proj(g):
        out.append(("k", 0))
    if n == AT_Q1 and has_proj(g):
        out.append(("q1", 0))
    if n == AT_Q and has_proj(g):
        out.append(("q", 0))
    if n == AT_V and has_max(g):
        out.append(("v", 0))
    if n == AT_OUT and has_out(g):
        out.append(("out", 0))
    if n == AT_T1 and tail(g):
        out.append(("t1", 0))
    if n == AT_MROW0 and has_max(g):
        out.append(("mrow", 0))
    if n == AT_T2 and tail(g) == "mid":
        out.append(("t2", 0))
    return out


def pv_slots(g, n):
    t = n - 2
    if t < 0:
        return [t] if has_out(g) else []
    if not has_b(g):
        return []
    return [] if t % 8 == 0 else [t - 1, t] if t % 8 == 1 else [t]


def per_iteration(g):
    b, m, a, o, t = has_b(g), has_max(g), has_proj(g), has_out(g), tail(g)
    return {
        "scores": 4 * SLOTS * b,
        "pv": sum(len(pv_slots(g, n)) for n in range(SLOTS)),
        "acc": 3 * b + o,
        "ring": len(ring_uses(g)),
        "max": 64 * m,
        "proj": 1 * a,
        "v": 1 * m,
        "mrow": b + m,
        "out": 1 * o,
        "tail": 1 * bool(t),
        "mid": 1 * (t == "mid"),
        "last": 1 * (t == "last"),
        "chain": (11 + 12 * (t != "")) * 0,
        "loads": 16 * (3 * has_proj(g) + 2 * has_max(g) + 2 * has_out(g)),
    }


G0 = -2
TOTAL = {g: {} for g in range(G0, STEPS + 4)}
for _name in per_iteration(0):
    _n = 0
    for _g in range(G0, STEPS + 4):
        TOTAL[_g][_name] = _n
        _n += per_iteration(_g)[_name]


def value(name, g, pair=None, add=0, times=1):
    v = times * TOTAL[g][name] + add
    if pair is None:
        return v
    return v + times * (TOTAL[g + 2][name] - TOTAL[g][name]) * pair


def wait(eng, sem, v):
    if not isinstance(v, int) or v > 0:
        eng.wait_ge(sem, v)


LOOPS = [(1, 4), (9, 10)]


def iterations(eng, body, first=G0, last=STEPS):
    g = first
    while g <= last:
        loop = next((l for l in LOOPS if l[0] == g), None)
        if loop:
            with eng.Fori(0, loop[1]) as pair:
                body(g, pair)
                body(g + 1, pair)
            g += 2 * loop[1]
        else:
            body(g, None)
            g += 1


def edges():
    first = 0
    out = []
    for c in range(NODES):
        n = min(c + 1, MAX_PREV)
        out.append((first + n - 1, first, first + n // 2))
        first += n
    return out


def preln_attention_cell(nc, x, Wq, bq, Wk, bk, Wv, bv, Wo, bo, ew, act_w, We, be, fWq, fWk, fWv, fWo, ln_g, ln_b, out):
    EDGES = edges()
    A_COLS = 3 * D + 3
    O_COLS = 2 * D + 1
    SETS = 2 + NODES

    def dram(name, shape, dt=F32):
        return nc.dram_tensor(name, shape, dt).ap()

    set_a = dram("set_a", [SETS, D, A_COLS])
    set_v = dram("set_v", [SETS, D, D])
    set_o = dram("set_o", [SETS, D, O_COLS])
    xt = dram("xt", [4 + 4 * NODES, D, S])
    resid = dram("resid", [2 * STEPS, D, S])
    x1_tok = dram("x1_tok", [B, 128, NB, D])
    parts_k = dram("parts_k", [2, 3, HEADS, DH, S], BF16)
    parts_q = dram("parts_q", [2, 3, HEADS, DH, S], BF16)
    dens = dram("dens", [2 * GROUP, S])
    rdens = dram("rdens", [2 * GROUP, S])
    mrows = dram("mrows", [2, 3, GROUP, S], BF16)

    with ExitStack() as ctx:
        def sb(name, shape, dt=F32):
            return ctx.enter_context(nc.sbuf_tensor(name, shape, dt))

        def psum(name, shape):
            return ctx.enter_context(nc.psum_tensor(name, shape, F32))

        def sem(name):
            return ctx.enter_context(nc.semaphore(name))

        k_aug = sb("k_aug", [128, 2, HEADS, S], BF16)
        q_aug = sb("q_aug", [128, 2, HEADS, S], BF16)
        probs = sb("probs", [128, PRING, GROUP, 512])
        v_sb = sb("v_sb", [128, 2, NB, HEADS, 32])
        xk = sb("xk", [128, S])
        xq = sb("xq", [128, S])
        xv = sb("xv", [128, S])
        w_a = sb("w_a", [128, A_COLS])
        w_v = sb("w_v", [128, D])
        w_o = sb("w_o", [128, O_COLS])
        q1 = sb("q1", [128, S])
        k32 = sb("k32", [128, S])
        q32 = sb("q32", [128, S])
        rest = sb("rest", [128, S])
        ksp = sb("ksp", [128, 3, S], BF16)
        qsp = sb("qsp", [128, 3, S], BF16)
        mx = sb("mx", [128, 2, NB, GROUP])
        mrest = sb("mrest", [128, 2, NB, GROUP])
        msp = sb("msp", [128, 2, NB, 3, GROUP], BF16)
        mrow_sb = sb("mrow_sb", [3 * GROUP, 2, S], BF16)
        ctx_t = sb("ctx_t", [128, 2, 2, S])
        den = sb("den", [128, 2 * GROUP * S // 128])
        rden = sb("rden", [128, 2 * GROUP * S // 128])
        rden_b = sb("rden_b", [128, 2, S])
        res_sb = sb("res_sb", [128, S])
        node_t = sb("node_t", [128, S])
        xtok = sb("xtok", [128, NB, D])
        xhat = sb("xhat", [128, NB, D])
        stats = sb("stats", [128, NB, 6])
        mv = sb("mv", [128, NB, 2])
        var = sb("var", [128, NB])
        rest_t = sb("rest_t", [128, S])
        sd = sb("sd", [128, NB])
        rstd = sb("rstd", [128, NB])
        ident = sb("ident", [128, 128])
        identb = sb("identb", [128, 128], BF16)
        gain = sb("gain", [128, D])
        shift = sb("shift", [128, D])

        sc = psum("sc", [128, 3, 512])
        ring = psum("ring", [128, 2, 2, 512])
        acc = psum("acc", [128, 512])

        raw = probs[:, :, :, :].rearrange("p a b c -> p (a b c)")[:, 0:(4 + 7 * NODES) * D].rearrange(
            "p (m d) -> p m d", d=D)
        prep = v_sb[:, :, :, :, :].rearrange("p a b c d -> p (a b c d)")
        st_a = q_aug[:, 0, :, :].rearrange("p a b -> p (a b)").bitcast(F32)[:, 0:SETS * A_COLS].rearrange(
            "p (s c) -> p s c", s=SETS)
        st_v = q_aug[:, 1, 0:2, :].rearrange("p a b -> p (a b)").bitcast(F32).rearrange("p (s c) -> p s c", s=SETS)
        st_o = q_aug[:, 1, 2:4, :].rearrange("p a b -> p (a b)").bitcast(F32)[:, 0:2 * O_COLS].rearrange(
            "p (s c) -> p s c", s=2)
        st_z = q_aug[:, 1, 4:8, :].rearrange("p a b -> p (a b)").bitcast(F32)[:, 0:NODES * O_COLS].rearrange(
            "p (s c) -> p s c", s=NODES)
        ones_col = prep[:, 2561:2562]
        wek_t, wev_t, wo_t = prep[:, 0:D], prep[:, D:2 * D], prep[:, 2 * D:3 * D]
        wo_c = prep[:, 3 * D:7 * D].rearrange("p (t j e) -> p t j e", t=4, j=4)
        ew_b = prep[:, 896:896 + 3 * NODES]
        aw_b = prep[:, 920:920 + NODES]
        be_c = prep[:, 928:928 + 20]
        be_rows = prep[0:20, 2688:2688 + D]
        bes = prep[:, 950:950 + 2 * NODES]
        vb = prep[:, 964:964 + NODES]
        bvo = prep[:, 972:974]
        bo_col = prep[:, 974:975]
        rows = prep[0:1, 1024:1024 + NODES * D]
        brow = prep[0:1, 2048:2048 + 4 * D].rearrange("p (w h c) -> p w h c", w=2, h=2)
        one = prep[0:1, 2560:2561]

        names = """prep_in prep_jobs prep_evac prep_made prep_stored prep_zero prep_ones prep_zeroed prep_cleared
            prep_id prep_x prep_norm prep_step ones_set consts
            scores_ready exp_done pv_done acc_ready acc_free ring_full ring_free0 ring_free1
            k_split q_split m_split k_step q_step m_step pool_tick dve_tick sp_tick
            mrow_dram mrow_loaded0 mrow_loaded1 parts_stored aug_loaded0 aug_loaded1
            den_stored den_loaded rden_done rden_stored rden_loaded ctx_done ctx_step q1_stored node_stored loaded x1_loaded
            tok_stored tok_step var_ready sd_done rstd_done xhat_done xt_stored final_step final_stored""".split()
        s = {n: sem(n) for n in names}
        ring_free = [s["ring_free0"], s["ring_free1"]]
        aug_loaded = [s["aug_loaded0"], s["aug_loaded1"]]
        mrow_loaded = [s["mrow_loaded0"], s["mrow_loaded1"]]
        block = ctx.enter_context(nc.Block())

        def ring_use(g, use):
            at = ring_uses(g).index(use)
            return at, (TOTAL[g]["ring"] + at) % 2

        def claim(pe, g, pair, use):
            at, r = ring_use(g, use)
            n = TOTAL[g]["ring"] + at
            v = n // 2
            if pair is not None:
                v = v + (TOTAL[g + 2]["ring"] - TOTAL[g]["ring"]) // 2 * pair
            wait(pe, ring_free[r], v)
            return ring[:, r]

        def filled(eng, g, pair, use):
            at, r = ring_use(g, use)
            eng.wait_ge(s["ring_full"], value("ring", g, pair, at + 1))
            return ring[:, r], ring_free[r]

        def evacuated(eng, g, pair, use):
            at, r = ring_use(g, use)
            v = (TOTAL[g]["ring"] + at) // 2 + 1
            if pair is not None:
                v = v + (TOTAL[g + 2]["ring"] - TOTAL[g]["ring"]) // 2 * pair
            eng.wait_ge(ring_free[r], v)
            if eng.engine == mybir.EngineType.SP and pair is not None:
                eng.sem_inc(s["sp_tick"], 1)

        def evacuated_before(eng, g, pair):
            n = TOTAL[g]["ring"] - 1
            v = n // 2 + 1
            if pair is not None:
                v = v + (TOTAL[g + 2]["ring"] - TOTAL[g]["ring"]) // 2 * pair
            eng.wait_ge(ring_free[n % 2], v)

        def flat(region):
            return region.rearrange("p a b -> p (a b)")

        JOBS = [("be", 0)] + [("wt", w) for w in range(3)] + [("bcol", 0), ("wo_t", 0), ("bo", 0)] + [("wo_c", t) for t in range(4)]
        JOBS += [(kind, c) for c in range(NODES) for kind in ("wek_t", "wev_t", "wkk", "wvv", "cols", "row")]
        JOBS += [(kind, b) for b in range(B) for kind in ("x_t", "xhat_t")]
        job_at = {j: n for n, j in enumerate(JOBS)}
        N_PREP_IN = 4 + 7 * NODES + 7 + 4
        N_STORED = 2 * B + 3 + 3 * NODES

        @block.sync
        def _(sp):
            n_in = 0

            def load(dst, src):
                nonlocal n_in
                sp.dma_start(dst, src).then_inc(s["prep_in"], 16)
                n_in += 1

            for n, w in enumerate((Wq, Wk, Wv, Wo)):
                load(raw[:, n, :], w)
            for c, (eq, ek, ev) in enumerate(EDGES):
                for n, w in enumerate((We[eq], We[ek], We[ev], fWq[c], fWk[c], fWv[c], fWo[c])):
                    load(raw[:, 4 + 7 * c + n, :], w)
            sp.wait_ge(s["prep_zero"], 1)
            load(be_rows, be)
            load(bvo[:, 0:1], bv.rearrange("(d o) -> d o", o=1))
            load(bvo[:, 1:2], bo.rearrange("(d o) -> d o", o=1))
            load(ew_b, ew.rearrange("(o c) w -> o (c w)", o=1).partition_broadcast(128))
            load(aw_b, act_w.rearrange("(o c) -> o c", o=1).partition_broadcast(128))
            load(gain[:, :], ln_g.rearrange("(o c) -> o c", o=1).partition_broadcast(128))
            load(shift[:, :], ln_b.rearrange("(o c) -> o c", o=1).partition_broadcast(128))
            for w, bias in enumerate((bq, bk)):
                for h in range(2):
                    load(brow[:, w, h, :].rearrange("p (a e) -> p a e", e=DH)[:, :, 0:8],
                         bias[64 * h:64 * h + 64].rearrange("(o a e) -> o a e", o=1, e=8))
            assert n_in == N_PREP_IN
            for b in range(B):
                if b:
                    sp.wait_ge(s["prep_evac"], job_at["x_t", b - 1] + 1)
                    sp.wait_ge(s["prep_norm"], b)
                sp.dma_start(xtok[:, :, :], x[b].rearrange("(k p) d -> p k d", p=128)).then_inc(s["prep_x"], 16)
                sp.wait_ge(s["prep_evac"], job_at["x_t", b] + 1)
                sp.dma_start(resid[2 * b], k32[:, :]).then_inc(s["prep_stored"], 16)
                sp.wait_ge(s["prep_evac"], job_at["xhat_t", b] + 1)
                sp.dma_start(xt[b], q32[:, :]).then_inc(s["prep_stored"], 16)
            sp.wait_ge(s["prep_made"], 1)
            sp.dma_start(set_a.rearrange("s p c -> p s c"), st_a).then_inc(s["prep_stored"], 16)
            sp.dma_start(set_v.rearrange("s p c -> p s c"), st_v).then_inc(s["prep_stored"], 16)
            sp.dma_start(set_o[0:2].rearrange("s p c -> p s c"), st_o).then_inc(s["prep_stored"], 16)
            for c in range(NODES):
                sp.dma_start(set_o[2 + c], st_z[:, c, :]).then_inc(s["prep_zeroed"], 16)
            sp.wait_ge(s["prep_zeroed"], 16 * NODES)
            for c in range(NODES):
                for hg in range(2):
                    sp.dma_start(set_o[2 + c, :, hg * D:hg * D + D].rearrange("(j e) o -> j e o", e=32)[:, 0:DH, :],
                                 fWo[c][64 * hg:64 * hg + 64, :].rearrange("(j d) o -> j d o", j=4)).then_inc(s["prep_stored"], 16)
                sp.dma_start(set_o[2 + c, DH:DH + 1, 0:D], rows[:, c * D:(c + 1) * D]).then_inc(s["prep_stored"], 16)
            sp.wait_ge(s["prep_stored"], 16 * N_STORED)

            def hold(eng, sem_, v):
                wait(eng, sem_, v)
                if not isinstance(v, int):
                    eng.sem_inc(s["sp_tick"], 1)

            def weight_set(step):
                if isinstance(step, int):
                    return step % 2 if step < ATTN_STEPS else 2 + (step - ATTN_STEPS) // B
                return (step - ATTN_STEPS) // B + 2

            def source(step, which):
                if isinstance(step, int) and step < ATTN_STEPS:
                    return step // 2
                t = step - ATTN_STEPS
                c, b = t // B, t % B
                if which == "q":
                    return t + 4
                if which == "k":
                    return (c + 3) // 8 * 4 + b + 4
                return (c + 1) // 2 * 4 + b + 4

            def loads_for(g, pair):
                if has_proj(g):
                    st = g + 2 if pair is None else pair * 2 + (g + 2)
                    sp.dma_start(xk[:, :], xt[source(st, "k")]).then_inc(s["loaded"], 16)
                    sp.dma_start(xq[:, :], xt[source(st, "q")]).then_inc(s["loaded"], 16)
                    sp.dma_start(w_a[:, :], set_a[weight_set(st)]).then_inc(s["loaded"], 16)
                if has_max(g):
                    st = g + 1 if pair is None else pair * 2 + (g + 1)
                    sp.dma_start(xv[:, :], xt[source(st, "v")]).then_inc(s["loaded"], 16)
                    sp.dma_start(w_v[:, :], set_v[weight_set(st)]).then_inc(s["loaded"], 16)
                if has_out(g):
                    st = g - 1 if pair is None else pair * 2 + (g - 1)
                    sp.dma_start(w_o[:, :], set_o[weight_set(st)]).then_inc(s["loaded"], 16)
                    at = st if g - 1 < ATTN_STEPS else st + STEPS
                    sp.dma_start(res_sb[:, :], resid[at]).then_inc(s["loaded"], 16)

            def aug_loads(g, hg):
                par = g % 2
                heads = slice(GROUP * hg, GROUP * hg + GROUP)
                src_k = parts_k[par][:, heads].rearrange("a h d t -> a d h t")
                src_q = parts_q[par][:, heads].rearrange("a h d t -> a d h t")
                for t, (pk, pq) in enumerate([(0, 0), (0, 1), (0, 2), (1, 0), (1, 1), (2, 0)]):
                    sp.dma_start(k_aug[DH * t:DH * t + DH, par, heads, :], src_k[pk]).then_inc(aug_loaded[hg], 16)
                    sp.dma_start(q_aug[DH * t:DH * t + DH, par, heads, :], src_q[pq]).then_inc(aug_loaded[hg], 16)

            def mrow_move(g, pair, hg, par, done, before):
                evacuated(sp, g, pair, ("mrow", hg))
                hold(sp, mrow_loaded[hg], before)
                sp.dma_start(mrows[hg].rearrange("a h t -> (a h) t"), mrow_sb[:, hg, :]).then_inc(s["mrow_dram"], 16)
                hold(sp, s["mrow_dram"], done * 16)
                sp.dma_start(q_aug[KR:KM, par, GROUP * hg:GROUP * hg + GROUP, :], mrows[hg]).then_inc(mrow_loaded[hg], 16)

            def mrow_loads(g, pair, hg):
                v = 16 * (g if hg else g + 1)
                return v if pair is None else pair * 32 + v

            def body(g, pair):
                par = g % 2
                if tail(g) == "last":
                    hold(sp, s["final_step"], value("last", g, pair, 0, 3))
                    sp.dma_start(res_tok, x1_tok[(g - 1) % B]).then_inc(s["x1_loaded"], 16)
                if has_out(g):
                    hold(sp, s["acc_free"], value("acc", g, pair, 1))
                    for hg in range(2):
                        for j in range(GROUP):
                            sp.dma_start(dens[GROUP * hg + j:GROUP * hg + j + 1, :],
                                         ctx_t[32 * j + DH:32 * j + DH + 1, 1 - par, hg, :]).then_inc(s["den_stored"], 16)
                    hold(sp, s["den_stored"], value("out", g, pair, 16 * 8, 16 * 8))
                    sp.dma_start(den[:, :], dens.rearrange("h (a t) -> (h a) t", a=16)).then_inc(s["den_loaded"], 16)
                if has_b(g):
                    mrow_move(g, pair, 1, par, value("mrow", g, pair, 1), mrow_loads(g, pair, 1))
                if has_out(g):
                    hold(sp, s["rden_done"], value("out", g, pair, 1))
                    sp.dma_start(rdens.rearrange("h (a t) -> (h a) t", a=16), rden[:, :]).then_inc(s["rden_stored"], 16)
                    hold(sp, s["rden_stored"], value("out", g, pair, 16, 16))
                    for j in range(GROUP):
                        src = rdens.rearrange("(g h) t -> h g t", g=2)[j:j + 1]
                        sp.dma_start(rden_b[32 * j:32 * j + 32, :, :], src.broadcast_to([32, 2, S])).then_inc(s["rden_loaded"], 16)
                if has_proj(g):
                    st = g + 2 if pair is None else pair * 2 + (g + 2)
                    evacuated(sp, g, pair, ("q1", 0))
                    sp.dma_start(resid[st + STEPS], q1[:, :]).then_inc(s["q1_stored"], 16)
                    hold(sp, s["k_split"], value("proj", g, pair, 1))
                    sp.dma_start(parts_k[par].rearrange("a h d t -> (h d) a t"), ksp[:, :, :]).then_inc(s["parts_stored"], 16)
                    hold(sp, s["q_split"], value("proj", g, pair, 1))
                    sp.dma_start(parts_q[par].rearrange("a h d t -> (h d) a t"), qsp[:, :, :]).then_inc(s["parts_stored"], 16)
                if has_out(g):
                    evacuated(sp, g, pair, ("out", 0))
                    st = g - 1 if pair is None else pair * 2 + (g - 1)
                    if tail(g) == "":
                        if g - 1 < ATTN_STEPS:
                            sp.dma_start(resid[st + 1], node_t[:, :]).then_inc(s["node_stored"], 16)
                        else:
                            sp.dma_start(xt[st], node_t[:, :]).then_inc(s["node_stored"], 16)
                if has_proj(g):
                    hold(sp, s["parts_stored"], value("proj", g, pair, 32, 32))
                    if has_b(g):
                        hold(sp, s["scores_ready"], value("scores", g, pair, 64))
                    aug_loads(g, 0)
                if has_max(g):
                    mrow_move(g, pair, 0, 1 - par, value("mrow", g, pair, 1 + has_b(g)), mrow_loads(g, pair, 0))
                if tail(g):
                    b = (g - 1) // 2 if pair is None else pair + (g - 1) // 2
                    if tail(g) == "mid":
                        evacuated(sp, g, pair, ("t1", 0))
                        sp.dma_start(x1_tok[b], xtok[:, :, :]).then_inc(s["tok_stored"], 16)
                        evacuated(sp, g, pair, ("t2", 0))
                        sp.dma_start(xt[b + 4], rest2).then_inc(s["xt_stored"], 16)
                    else:
                        hold(sp, s["final_step"], value("last", g, pair, 3, 3))
                        sp.dma_start(out[(g - 1) % B].rearrange("(k p) d -> p k d", p=128), xhat[:, :, :]).then_inc(s["final_stored"], 16)
                if g < STEPS:
                    n = g + 1
                    if has_proj(g):
                        evacuated(sp, g, pair, ("q", 0))
                        hold(sp, s["q1_stored"], value("proj", g, pair, 16, 16))
                    if has_max(g):
                        evacuated(sp, g, pair, ("v", 0))
                    if has_out(g):
                        evacuated(sp, g, pair, ("out", 0))
                    if has_out(g) and tail(g) == "":
                        hold(sp, s["node_stored"], node_value(g, pair))
                    if tail(g) == "mid":
                        hold(sp, s["xt_stored"], value("mid", g, pair, 16, 16))
                        hold(sp, s["tok_stored"], value("mid", g, pair, 16, 16))
                    loads_for(n, pair)
                if has_proj(g):
                    if has_b(g):
                        hold(sp, s["scores_ready"], value("scores", g, pair, 128))
                    aug_loads(g, 1)

            def node_value(g, pair):
                n = sum(1 for i in range(G0, g + 1) if has_out(i) and tail(i) == "")
                if pair is None:
                    return 16 * n
                per = sum(1 for i in (g + 1, g + 2) if has_out(i) and tail(i) == "")
                return 16 * n + 16 * per * pair

            rest2 = rest_t[:, :]
            res_tok = rest_t[:, :].rearrange("p (k d) -> p k d", k=NB)
            loads_for(G0, None)
            for g in range(G0, LOOPS[1][0]):
                body(g, None)
            iterations(sp, body, LOOPS[1][0])
            hold(sp, s["final_stored"], 16 * B)
            hold(sp, s["node_stored"], node_value(STEPS, None))
            hold(sp, s["mrow_dram"], value("mrow", STEPS, None, 0, 16))

        @block.tensor
        def _(pe):
            pe.wait_ge(s["prep_id"], 3)
            pe.wait_ge(s["prep_in"], 16 * N_PREP_IN)
            for n, (kind, i) in enumerate(JOBS):
                region = ring[:, n % 2]
                out1 = region[:, 0, 0:D]
                after = n - 1
                base = 4 + 7 * i
                if kind == "be":
                    last = pe.transpose(out1[:, 0:20], be_rows, ident[0:20, 0:20])
                elif kind == "wt":
                    wait(pe, s["prep_evac"], after)
                    last = pe.transpose(out1, raw[:, i, :], ident[:, :])
                elif kind == "bcol":
                    wait(pe, s["prep_evac"], after)
                    for w in range(2):
                        for h in range(2):
                            last = pe.matmul(region[:, 0, 2 * w + h:2 * w + h + 1], brow[:, w, h, :], one, start=True, stop=True)
                elif kind == "wo_t":
                    pe.wait_ge(s["prep_evac"], after)
                    last = pe.transpose(out1, raw[:, 3, :], ident[:, :])
                elif kind == "bo":
                    pe.wait_ge(s["prep_evac"], n)
                    last = pe.matmul(out1[:, 0:1], wo_t, bvo[:, 0:1], start=True, stop=True)
                elif kind == "wo_c":
                    pe.wait_ge(s["prep_evac"], after)
                    pe.wait_ge(s["prep_step"], 2)
                    last = pe.transpose(out1, wo_c[:, i].rearrange("p j e -> p (j e)"), ident[:, :])
                elif kind in ("wek_t", "wev_t"):
                    pe.wait_ge(s["prep_evac"], after)
                    last = pe.transpose(out1, raw[:, base + (1 if kind == "wek_t" else 2), :], ident[:, :])
                elif kind in ("wkk", "wvv"):
                    pe.wait_ge(s["prep_evac"], n)
                    w, at = (wek_t, 4) if kind == "wkk" else (wev_t, 5)
                    last = pe.matmul(out1, w, raw[:, base + at, :], start=True, stop=True)
                elif kind == "cols":
                    pe.wait_ge(s["prep_evac"], after)
                    pe.matmul(out1[:, 0:1], raw[:, base + 4, :], bes[:, 2 * i:2 * i + 1], start=True, stop=True)
                    last = pe.matmul(out1[:, 1:2], raw[:, base + 5, :], bes[:, 2 * i + 1:2 * i + 2], start=True, stop=True)
                elif kind == "row":
                    pe.wait_ge(s["prep_evac"], n)
                    last = pe.matmul(out1[0:1, :], vb[:, i:i + 1], raw[:, base + 6, :], start=True, stop=True)
                else:
                    if kind == "x_t":
                        pe.wait_ge(s["prep_evac"], after)
                        pe.wait_ge(s["prep_x"], 16 * (i + 1))
                        src = xtok
                    else:
                        pe.wait_ge(s["prep_evac"], after)
                        pe.wait_ge(s["prep_norm"], i + 1)
                        src = xhat
                    for k in range(NB):
                        last = pe.transpose(region[:, k // 4, 128 * (k % 4):128 * (k % 4) + 128], src[:, k, :], ident[:, :])
                last.then_inc(s["prep_jobs"], 1)
            pe.wait_ge(s["prep_evac"], len(JOBS))
            pe.wait_ge(s["consts"], 1)
            pe.wait_ge(s["ones_set"], 2)

            def project(g, pair, use, w, src, ready=None):
                region = claim(pe, g, pair, use)
                for half in range(2):
                    last = pe.matmul(region[:, half, :], w, src[:, 512 * half:512 * half + 512], start=True, stop=True)
                last.then_inc(s["ring_full"], 1)

            def chore(g, pair, use):
                kind, hg = use
                if kind == "k":
                    pe.wait_ge(s["loaded"], value("loads", g + 1, pair))
                    project(g, pair, use, w_a[:, 2 * D:3 * D], xk)
                elif kind == "q1":
                    project(g, pair, use, w_a[:, 0:D], xq)
                elif kind == "q":
                    evacuated(pe, g, pair, ("q1", 0))
                    project(g, pair, use, w_a[:, D:2 * D], q1)
                elif kind == "v":
                    pe.wait_ge(s["loaded"], value("loads", g + 1, pair))
                    region = claim(pe, g, pair, use)
                    for k in range(NB):
                        last = pe.matmul(region[:, k // 4, 128 * (k % 4):128 * (k % 4) + 128],
                                         xv[:, 128 * k:128 * k + 128], w_v[:, :], start=True, stop=True)
                    last.then_inc(s["ring_full"], 1)
                elif kind == "mrow":
                    done = value("mrow", g, pair, 1 if hg else 1 + has_b(g))
                    pe.wait_ge(s["m_split"], done)
                    region = claim(pe, g, pair, use)
                    for k in range(NB):
                        last = pe.matmul(region[0:3 * GROUP, k // 4, 128 * (k % 4):128 * (k % 4) + 128],
                                         msp[:, hg, k].rearrange("p a h -> p (a h)"), identb[:, :], start=True, stop=True)
                    last.then_inc(s["ring_full"], 1)
                elif kind == "out":
                    pe.wait_ge(s["loaded"], value("loads", g + 1, pair))
                    pe.wait_ge(s["ctx_done"], value("out", g, pair, 1))
                    region = claim(pe, g, pair, use)
                    for half in range(2):
                        for hg2 in range(2):
                            last = pe.matmul(region[:, half, :], w_o[:, D * hg2:D * hg2 + D],
                                             ctx_t[:, (g - 1) % 2, hg2, 512 * half:512 * half + 512], start=hg2 == 0, stop=hg2 == 1)
                    last.then_inc(s["ring_full"], 1)
                else:
                    if kind == "t1":
                        evacuated(pe, g, pair, ("out", 0))
                    else:
                        pe.wait_ge(s["xhat_done"], value("tail", g, pair, 1))
                    region = claim(pe, g, pair, use)
                    for k in range(NB):
                        src = node_t[:, 128 * k:128 * k + 128] if kind == "t1" else xhat[:, k, :]
                        last = pe.transpose(region[:, k // 4, 128 * (k % 4):128 * (k % 4) + 128], src, ident[:, :])
                    last.then_inc(s["ring_full"], 1)

            def score(g, pair, n, j):
                i = 4 * n + j
                before = i - 2 if i >= 3 else (-1, 0, -2)[i]
                wait(pe, s["exp_done"], value("scores", g, pair, before))
                hg, qh, kc = n // 16, n // 8 % 2, n % 8
                h = GROUP * hg + j
                pe.matmul(sc[:, i % 3, :], k_aug[0:KM, g % 2, h, 128 * kc:128 * kc + 128],
                          q_aug[0:KM, g % 2, h, 512 * qh:512 * qh + 512], start=True, stop=True).then_inc(s["scores_ready"], 1)

            def max_scores(g, pair, u):
                hg, qb, h = u // 32, u % 32 // 4, u // 32 * GROUP + u % 4
                region = claim(pe, g, pair, ("max", u))
                par = (g + 1) % 2
                for half in range(2):
                    last = pe.matmul(region[:, half, :], q_aug[0:KR, par, h, 128 * qb:128 * qb + 128],
                                     k_aug[0:KR, par, h, 512 * half:512 * half + 512], start=True, stop=True)
                last.then_inc(s["ring_full"], 1)

            def pv(g, pair, t):
                par, t_in = (g % 2, t) if t >= 0 else ((g - 1) % 2, t + SLOTS)
                hg, kc = t_in // 16, t_in % 8
                pe.wait_ge(s["exp_done"], value("scores", g, pair, 4 * (t + 1)))
                if kc == 0:
                    wait(pe, s["acc_free"], value("acc", g, pair, t_in // 8 + has_out(g)))
                for j in range(GROUP):
                    last = pe.matmul(acc[32 * j:32 * j + 32, :], v_sb[:, par, kc, GROUP * hg + j, :],
                                     probs[:, t_in % PRING, j, :], start=kc == 0, stop=kc == 7)
                last.then_inc(s["pv_done"], 1)

            def body(g, pair):
                for n in range(SLOTS):
                    for use in chores(g, n):
                        chore(g, pair, use)
                    if has_max(g) and n % 16 == 0:
                        pe.wait_ge(aug_loaded[n // 16], aug_value(g, pair))
                    if has_b(g) and n % 16 == 0:
                        pe.wait_ge(mrow_loaded[n // 16], mrow_value(g, pair))
                    for half in range(2):
                        if has_b(g):
                            score(g, pair, n, 2 * half)
                            score(g, pair, n, 2 * half + 1)
                        if has_max(g):
                            max_scores(g, pair, 2 * n + half)
                    for t in pv_slots(g, n):
                        pv(g, pair, t)

            def aug_value(g, pair):
                v = 16 * 2 * TERMS * (g + 2)
                return v if pair is None else v + 16 * 2 * TERMS * 2 * pair

            def mrow_value(g, pair):
                return 16 * (g + 1) if pair is None else pair * 32 + 16 * (g + 1)

            iterations(pe, body)

        @block.scalar
        def _(act):
            for b in range(B):
                act.wait_ge(s["var_ready"], b + 1)
                act.activation(sd[:, :], var[:, :], ACT.Sqrt).then_inc(s["sd_done"], 1)
            act.wait_ge(s["prep_evac"], len(JOBS))
            act.wait_ge(s["prep_stored"], 16 * N_STORED)

            def chore(g, pair, use):
                kind, hg = use
                if kind == "k":
                    region, free = filled(act, g, pair, use)
                    wait(act, s["k_split"], value("proj", g, pair))
                    act.activation(k32[:, :], flat(region), ACT.Identity, bias=w_a[:, 3 * D + 2:3 * D + 3]).then_inc(free, 1)
                elif kind == "q1":
                    region, free = filled(act, g, pair, use)
                    if g > G0:
                        act.wait_ge(s["q1_stored"], value("proj", g, pair, 0, 16))
                    act.activation(q1[:, :], flat(region), ACT.Identity, bias=w_a[:, 3 * D:3 * D + 1]).then_inc(free, 1)
                elif kind == "q":
                    region, free = filled(act, g, pair, use)
                    wait(act, s["q_split"], value("proj", g, pair))
                    act.activation(q32[:, :], flat(region), ACT.Identity, bias=w_a[:, 3 * D + 1:3 * D + 2]).then_inc(free, 1)
                elif kind == "v":
                    region, free = filled(act, g, pair, use)
                    if has_out(g):
                        act.wait_ge(s["pv_done"], value("pv", g, pair, 2))
                    act.activation(v_sb[:, (g + 1) % 2].rearrange("p k h e -> p (k h) e")[:, :, 0:DH],
                                   flat(region).rearrange("p (a e) -> p a e", e=DH), ACT.Copy).then_inc(free, 1)
                elif kind == "mrow":
                    region, free = filled(act, g, pair, use)
                    wait(act, s["mrow_dram"], value("mrow", g, pair, (0 if hg else int(has_b(g))) * 16 - 16, 16))
                    act.activation(mrow_sb[:, hg, :], flat(region)[0:3 * GROUP, :], ACT.Copy).then_inc(free, 1)
                elif kind == "t2":
                    region, free = filled(act, g, pair, use)
                    act.activation(rest_t[:, :], flat(region), ACT.Copy).then_inc(free, 1)

            def body(g, pair):
                for n in range(SLOTS):
                    for use in chores(g, n):
                        chore(g, pair, use)
                    if n == AT_DEN and has_out(g):
                        context(g, pair, (g - 1) % 2, 3, 2, 0)
                    if n in (10, 18, 26) and has_b(g):
                        q = n // 8 - 1
                        context(g, pair, g % 2, q, 8 * (q + 1) + 2 * has_out(g), q + has_out(g))
                    if has_b(g):
                        if n >= PRING or has_out(g):
                            act.wait_ge(s["pv_done"], value("pv", g, pair, n - PRING + 1 + 2 * has_out(g)))
                        for j in range(GROUP):
                            i = 4 * n + j
                            act.wait_ge(s["scores_ready"], value("scores", g, pair, i + 1))
                            act.activation(probs[:, n % PRING, j, :], sc[:, i % 3, :], ACT.Exp).then_inc(s["exp_done"], 1)
                    if tail(g) and n == AT_T1 + 6:
                        act.wait_ge(s["var_ready"], value("tail", g, pair, B + 1))
                        act.activation(sd[:, :], var[:, :], ACT.Sqrt).then_inc(s["sd_done"], 1)

            def context(g, pair, par, q, pvs, nth):
                act.wait_ge(s["pv_done"], value("pv", g, pair, pvs))
                act.activation(ctx_t[:, par, q // 2, 512 * (q % 2):512 * (q % 2) + 512], acc[:, :],
                               ACT.Copy).then_inc(s["acc_free"], 1)

            iterations(act, body)

        @block.gpsimd
        def _(pool):
            pool.memset(ident[:, :], 0.0).then_inc(s["prep_id"], 1)
            pool.wait_ge(s["prep_id"], 1)
            pool.affine_select(out=ident[:, :], in_=ident[:, :], compare_op=ALU.not_equal, fill=1.0, base=0,
                               pattern=[[-1, 128]], channel_multiplier=1).then_inc(s["prep_id"], 1)
            pool.wait_ge(s["prep_id"], 2)
            pool.tensor_copy(identb[:, :], ident[:, :]).then_inc(s["prep_id"], 1)
            pool.wait_ge(s["prep_id"], 3)
            pool.memset(k_aug[KR:KM, :, :, :], -1.0).then_inc(s["consts"], 1)
            pool.wait_ge(s["prep_evac"], len(JOBS))
            pool.wait_ge(s["prep_stored"], 16 * N_STORED)
            for par in range(2):
                pool.wait_ge(s["consts"], 1) if par == 0 else pool.wait_ge(s["ones_set"], 1)
                pool.memset(v_sb[:, par].rearrange("p k h e -> p (k h) e")[:, :, DH:32], 1.0).then_inc(s["ones_set"], 1)

            def split(src, parts, tmp, step, first, done):
                pool.sem_inc(s["pool_tick"], 1)
                pool.tensor_copy(parts[0], src).then_inc(step, 1)
                pool.wait_ge(step, first + 1)
                pool.tensor_tensor(tmp, src, parts[0], ALU.subtract).then_inc(step, 1)
                pool.wait_ge(step, first + 2)
                pool.sem_inc(s["pool_tick"], 1)
                pool.tensor_copy(parts[1], tmp).then_inc(step, 1)
                pool.wait_ge(step, first + 3)
                pool.tensor_tensor(parts[2], tmp, parts[1], ALU.subtract).then_inc(done, 1)

            def m_split(g, pair, hg, nth):
                if hg:
                    evacuated_before(pool, g, pair)
                else:
                    evacuated(pool, g, pair, ("max", 31))
                split(mx[:, hg], [msp[:, hg, :, a, :] for a in range(3)], mrest[:, hg], s["m_step"],
                      value("mrow", g, pair, 3 * nth, 3), s["m_split"])

            pool.wait_ge(s["ones_set"], 2)

            def context(g, pair):
                wait(pool, s["k_split"], value("proj", g, pair, int(has_proj(g))))
                pool.wait_ge(s["rden_loaded"], value("out", g, pair, 16 * GROUP, 16 * GROUP))
                part = ctx_t[:, (g - 1) % 2, :, :]
                pool.tensor_tensor(part, part, rden_b[:, :, :], ALU.mult).then_inc(s["ctx_done"], 1)

            def body(g, pair):
                if has_b(g):
                    m_split(g, pair, 1, 0)
                if has_proj(g):
                    for use, src, parts, step, done in (("k", k32, ksp, "k_step", "k_split"), ("q", q32, qsp, "q_step", "q_split")):
                        evacuated(pool, g, pair, (use, 0))
                        if g > G0:
                            pool.wait_ge(s["parts_stored"], value("proj", g, pair, 0, 32))
                        if use == "q":
                            pool.wait_ge(s["k_split"], value("proj", g, pair, 1))
                            if has_out(g):
                                pool.wait_ge(s["ctx_done"], value("out", g, pair, 1))
                        split(src[:, :], [parts[:, a, :] for a in range(3)], rest[:, :], s[step],
                              value("proj", g, pair, 0, 3), s[done])
                        if use == "k" and has_out(g):
                            context(g, pair)
                elif has_out(g):
                    context(g, pair)
                if has_max(g):
                    m_split(g, pair, 0, int(has_b(g)))

            iterations(pool, body)

        @block.vector
        def _(dve):
            dve.memset(prep[:, :], 0.0).then_inc(s["prep_zero"], 1)
            dve.memset(q_aug[:, :, :, :].rearrange("p a b c -> p (a b c)").bitcast(F32), 0.0).then_inc(s["prep_cleared"], 1)
            dve.wait_ge(s["prep_zero"], 1)
            dve.wait_ge(s["prep_cleared"], 1)
            dve.memset(prep[:, 2560:2562], 1.0).then_inc(s["prep_step"], 1)
            dve.wait_ge(s["prep_id"], 2)
            dve.wait_ge(s["prep_in"], 16 * N_PREP_IN)
            dve.wait_ge(s["prep_step"], 1)
            for h in range(2):
                dve.tensor_copy(st_a[:, h, 0:D], ident[:, :])
                dve.tensor_copy(st_o[:, h, 2 * D:], ones_col)
            for c, (eq, ek, ev) in enumerate(EDGES):
                base = 4 + 7 * c
                dve.tensor_scalar(st_a[:, 2 + c, 0:D], raw[:, base, :], ew_b[:, 3 * c:3 * c + 1], None, ALU.mult)
                dve.tensor_copy(st_z[:, c, 2 * D:], aw_b[:, c:c + 1])
                dve.tensor_scalar(st_a[:, 2 + c, D:2 * D], raw[:, base + 3, :], DH ** -0.5, None, ALU.mult)
            for t in range(4):
                last = dve.tensor_copy(wo_c[:, t, :, 0:8], raw[:, 3, 32 * t:32 * t + 32].rearrange("p (j e) -> p j e", e=8))
            last.then_inc(s["prep_step"], 1)
            factor = 8 ** -0.5
            for n, (kind, i) in enumerate(JOBS):
                region = ring[:, n % 2]
                out1 = region[:, 0, 0:D]
                if kind == "x_t":
                    dve.wait_ge(s["prep_x"], 16 * (i + 1))
                    for k in range(NB):
                        last = dve.bn_stats(stats[:, k, :], xtok[:, k, :])
                    last.then_inc(s["prep_step"], 1)
                    dve.wait_ge(s["prep_step"], 3 + 3 * i)
                    for k in range(NB):
                        last = dve.bn_aggr(mv[:, k, :], stats[:, k, :])
                    last.then_inc(s["prep_step"], 1)
                    dve.wait_ge(s["prep_step"], 4 + 3 * i)
                    dve.tensor_scalar(var[:, :], mv[:, :, 1], 1e-5, None, ALU.add).then_inc(s["var_ready"], 1)
                    dve.wait_ge(s["sd_done"], i + 1)
                    dve.reciprocal(rstd[:, :], sd[:, :]).then_inc(s["prep_step"], 1)
                    dve.wait_ge(s["prep_step"], 5 + 3 * i)
                    for k in range(NB):
                        last = dve.tensor_scalar(xhat[:, k, :], xtok[:, k, :], mv[:, k, 0:1], rstd[:, k:k + 1], ALU.subtract, ALU.mult)
                    last.then_inc(s["prep_norm"], 1)
                dve.wait_ge(s["prep_jobs"], n + 1)
                if kind == "be":
                    for c, edge in enumerate(EDGES):
                        for w, dst in ((1, bes[:, 2 * c:2 * c + 1]), (2, bes[:, 2 * c + 1:2 * c + 2]),
                                       (0, st_a[:, 2 + c, 3 * D:3 * D + 1])):
                            e = edge[w]
                            last = dve.tensor_scalar(dst, out1[:, e:e + 1], ew_b[:, 3 * c + w:3 * c + w + 1], None, ALU.mult)
                elif kind == "wt":
                    for h in range(2):
                        src = out1[:, 64 * h:64 * h + 64].rearrange("p (a e) -> p a e", e=8)
                        if i == 2:
                            dst = st_v[:, h, :]
                        else:
                            dst = st_a[:, h, D * (1 + i):D * (2 + i)]
                        last = dve.tensor_scalar(dst.rearrange("p (a e) -> p a e", e=DH)[:, :, 0:8], src,
                                                 factor if i == 0 else 1.0, None, ALU.mult)
                elif kind == "bcol":
                    for w in range(2):
                        for h in range(2):
                            last = dve.tensor_scalar(st_a[:, h, 3 * D + 1 + w:3 * D + 2 + w], region[:, 0, 2 * w + h:2 * w + h + 1],
                                                     1.0 if w else factor, None, ALU.mult)
                elif kind == "wo_t":
                    last = dve.tensor_copy(wo_t, out1)
                elif kind == "bo":
                    dve.wait_ge(s["prep_step"], 2)
                    last = dve.tensor_tensor(wo_c[:, 2, 0, DH:DH + 1], out1[:, 0:1], bvo[:, 1:2], ALU.add)
                elif kind == "wo_c":
                    last = dve.tensor_copy(st_o[:, i // 2, D * (i % 2):D * (i % 2) + D], out1)
                elif kind == "wek_t":
                    last = dve.tensor_scalar(wek_t, out1, ew_b[:, 3 * i + 1:3 * i + 2], None, ALU.mult)
                elif kind == "wev_t":
                    last = dve.tensor_scalar(wev_t, out1, ew_b[:, 3 * i + 2:3 * i + 3], None, ALU.mult)
                elif kind == "wkk":
                    last = dve.tensor_copy(st_a[:, 2 + i, 2 * D:3 * D], out1)
                elif kind == "wvv":
                    last = dve.tensor_copy(st_v[:, 2 + i, :], out1)
                elif kind == "cols":
                    dve.tensor_copy(st_a[:, 2 + i, 3 * D + 2:3 * D + 3], out1[:, 0:1])
                    last = dve.tensor_copy(vb[:, i:i + 1], out1[:, 1:2])
                elif kind == "row":
                    last = dve.tensor_copy(rows[:, i * D:(i + 1) * D], out1[0:1, :])
                elif kind == "x_t":
                    wait(dve, s["prep_stored"], 32 * i)
                    last = dve.tensor_copy(k32[:, :], flat(region))
                else:
                    last = dve.tensor_copy(q32[:, :], flat(region))
                last.then_inc(s["prep_evac"], 1)
            dve.sem_inc(s["prep_made"], 1)

            def tail_part(g, pair, n):
                k0 = n - AT_T1
                if k0 == 0:
                    region, free = filled(dve, g, pair, ("t1", 0))
                    dve.tensor_copy(xtok[:, :, :].rearrange("p k d -> p (k d)"), flat(region)).then_inc(free, 1)
                elif 1 <= k0 <= 4:
                    if k0 == 1:
                        evacuated(dve, g, pair, ("t1", 0))
                    for k in (2 * k0 - 2, 2 * k0 - 1):
                        last = dve.bn_stats(stats[:, k, :], xtok[:, k, :])
                    if k0 == 4:
                        last.then_inc(s["tok_step"], 1)
                elif k0 == 5:
                    dve.wait_ge(s["tok_step"], value("tail", g, pair, 1, 2))
                    dve.sem_inc(s["dve_tick"], 1)
                    for k in range(NB):
                        last = dve.bn_aggr(mv[:, k, :], stats[:, k, :])
                    last.then_inc(s["tok_step"], 1)
                    dve.wait_ge(s["tok_step"], value("tail", g, pair, 2, 2))
                    dve.tensor_scalar(var[:, :], mv[:, :, 1], 1e-5 if tail(g) == "mid" else 1e-6, None,
                                      ALU.add).then_inc(s["var_ready"], 1)
                elif k0 == 8:
                    dve.wait_ge(s["sd_done"], value("tail", g, pair, B + 1))
                    dve.reciprocal(rstd[:, :], sd[:, :]).then_inc(s["rstd_done"], 1)
                    dve.wait_ge(s["rstd_done"], value("tail", g, pair, 1))
                    if tail(g) == "last":
                        wait(dve, s["final_stored"], value("last", g, pair, 0, 16))
                    for k in range(NB):
                        last = dve.tensor_scalar(xhat[:, k, :], xtok[:, k, :], mv[:, k, 0:1], rstd[:, k:k + 1], ALU.subtract, ALU.mult)
                    last.then_inc(s["xhat_done"], 1)
                elif k0 == 10 and tail(g) == "last":
                    dve.wait_ge(s["xhat_done"], value("tail", g, pair, 1))
                    dve.tensor_tensor(xhat[:, :, :], xhat[:, :, :], gain[:, :].rearrange("p (o d) -> p o d", o=1).broadcast_to([128, NB, D]),
                                      ALU.mult).then_inc(s["final_step"], 1)
                    dve.wait_ge(s["final_step"], value("last", g, pair, 1, 3))
                    dve.tensor_tensor(xhat[:, :, :], xhat[:, :, :], shift[:, :].rearrange("p (o d) -> p o d", o=1).broadcast_to([128, NB, D]),
                                      ALU.add).then_inc(s["final_step"], 1)
                    dve.wait_ge(s["final_step"], value("last", g, pair, 2, 3))
                    dve.wait_ge(s["x1_loaded"], value("last", g, pair, 16, 16))
                    dve.tensor_tensor(xhat[:, :, :], xhat[:, :, :], rest_t[:, :].rearrange("p (k d) -> p k d", k=NB),
                                      ALU.add).then_inc(s["final_step"], 1)

            def body(g, pair):
                for n in range(SLOTS):
                    if n == AT_OUT and has_out(g):
                        region, free = filled(dve, g, pair, ("out", 0))
                        dve.scalar_tensor_tensor(node_t[:, :], flat(region), w_o[:, 2 * D:2 * D + 1], res_sb[:, :],
                                                 ALU.mult, ALU.add).then_inc(free, 1)
                    if n == AT_RDEN and has_out(g):
                        dve.wait_ge(s["den_loaded"], value("out", g, pair, 16, 16))
                        dve.reciprocal(rden[:, :], den[:, :]).then_inc(s["rden_done"], 1)
                    if tail(g):
                        tail_part(g, pair, n)
                    if has_max(g):
                        for u in (2 * n, 2 * n + 1):
                            region, free = filled(dve, g, pair, ("max", u))
                            dve.tensor_reduce(mx[:, u // 32, u % 32 // 4, u % 4:u % 4 + 1], region, AX.XY, ALU.max).then_inc(free, 1)

            iterations(dve, body)


_INS = ["L0_attn_x", "L0_attn_Wq", "L0_attn_bq", "L0_attn_Wk", "L0_attn_bk", "L0_attn_Wv", "L0_attn_bv", "L0_attn_Wo",
        "L0_attn_bo", "L0_ffn_ew", "L0_ffn_act_w", "L0_ffn_We", "L0_ffn_be", "L0_ffn_Wq", "L0_ffn_Wk", "L0_ffn_Wv",
        "L0_ffn_Wo", "L0_ffn_ln_g", "L0_ffn_ln_b"]


def kernel(**inputs):
    import numpy as np
    import concourse.bacc as bacc
    from concourse.bass_utils import run_bass_kernel_spmd

    nc = bacc.Bacc("TRN2", target_bir_lowering=False, num_devices=1)
    arrays, args = {}, []
    for name in _INS:
        a = np.ascontiguousarray(inputs[name])
        arrays[f"in_{name}"] = a
        args.append(nc.dram_tensor(f"in_{name}", a.shape, mybir.dt.from_np(a.dtype), kind="ExternalInput").ap())
    out = nc.dram_tensor("out", (B, S, D), F32, kind="ExternalOutput").ap()
    preln_attention_cell(nc, *args, out)
    r = run_bass_kernel_spmd(nc, [arrays], core_ids=[0])
    return r.results[0]["out"]
```

```python
from contextlib import ExitStack

import concourse.bass as bass
from concourse import mybir

F32 = mybir.dt.float32
BF16 = mybir.dt.bfloat16
ALU = mybir.AluOpType
ACT = mybir.ActivationFunctionType
AX = mybir.AxisListType

D = 128
B = 4
S = 1024
NODES = 6
MAX_PREV = 5
HEADS = 8
DH = 16
TERMS = 6
KR = TERMS * DH
KM = KR + 3
GROUP = 4
NB = S // 128
ATTN_STEPS = 2 * B
STEPS = ATTN_STEPS + NODES * B
SLOTS = 32
PRING = 4

AT_MROW1, AT_K, AT_Q1, AT_Q, AT_V, AT_OUT, AT_T1, AT_MROW0, AT_T2 = 1, 2, 4, 6, 11, 14, 17, 19, 29
AT_DEN, AT_RDEN = 2, 8


def has_b(g):
    return 0 <= g < STEPS


def has_max(g):
    return 0 <= g + 1 < STEPS


def has_proj(g):
    return 0 <= g + 2 < STEPS


def has_out(g):
    return 0 <= g - 1 < STEPS


def tail(g):
    s = g - 1
    if 0 <= s < ATTN_STEPS:
        return "mid" if s % 2 else ""
    return "last" if STEPS - B <= s < STEPS else ""


def ring_uses(g):
    uses = []
    for n in range(SLOTS):
        tiles = [[("max", 2 * n)], [("max", 2 * n + 1)]] if has_max(g) else [[], []]
        uses += tiles[0] + chores(g, n) + tiles[1]
    return uses


def chores(g, n):
    out = []
    if n == AT_MROW1 and has_b(g):
        out.append(("mrow", 1))
    if n == AT_K and has_proj(g):
        out.append(("k", 0))
    if n == AT_Q1 and has_proj(g):
        out.append(("q1", 0))
    if n == AT_Q and has_proj(g):
        out.append(("q", 0))
    if n == AT_V and has_max(g):
        out.append(("v", 0))
    if n == AT_OUT and has_out(g):
        out.append(("out", 0))
    if n == AT_T1 and tail(g):
        out.append(("t1", 0))
    if n == AT_MROW0 and has_max(g):
        out.append(("mrow", 0))
    if n == AT_T2 and tail(g) == "mid":
        out.append(("t2", 0))
    return out


def pv_slots(g, n):
    t = n - 2
    return [t] if (has_b(g) if t >= 0 else has_out(g)) else []


def per_iteration(g):
    b, m, a, o, t = has_b(g), has_max(g), has_proj(g), has_out(g), tail(g)
    return {
        "scores": 4 * SLOTS * b,
        "pv": sum(len(pv_slots(g, n)) for n in range(SLOTS)),
        "acc": 3 * b + o,
        "ring": len(ring_uses(g)),
        "max": 64 * m,
        "proj": 1 * a,
        "v": 1 * m,
        "mrow": b + m,
        "out": 1 * o,
        "tail": 1 * bool(t),
        "mid": 1 * (t == "mid"),
        "last": 1 * (t == "last"),
        "chain": (11 + 12 * (t != "")) * 0,
        "loads": 16 * (3 * has_proj(g) + 2 * has_max(g) + 2 * has_out(g)),
    }


G0 = -2
TOTAL = {g: {} for g in range(G0, STEPS + 4)}
for _name in per_iteration(0):
    _n = 0
    for _g in range(G0, STEPS + 4):
        TOTAL[_g][_name] = _n
        _n += per_iteration(_g)[_name]


def value(name, g, pair=None, add=0, times=1):
    v = times * TOTAL[g][name] + add
    if pair is None:
        return v
    return v + times * (TOTAL[g + 2][name] - TOTAL[g][name]) * pair


def wait(eng, sem, v):
    if not isinstance(v, int) or v > 0:
        eng.wait_ge(sem, v)


LOOPS = [(1, 4), (9, 10)]


def iterations(eng, body, first=G0, last=STEPS):
    g = first
    while g <= last:
        loop = next((l for l in LOOPS if l[0] == g), None)
        if loop:
            with eng.Fori(0, loop[1]) as pair:
                body(g, pair)
                body(g + 1, pair)
            g += 2 * loop[1]
        else:
            body(g, None)
            g += 1


def edges():
    first = 0
    out = []
    for c in range(NODES):
        n = min(c + 1, MAX_PREV)
        out.append((first + n - 1, first, first + n // 2))
        first += n
    return out


def preln_attention_cell(nc, x, Wq, bq, Wk, bk, Wv, bv, Wo, bo, ew, act_w, We, be, fWq, fWk, fWv, fWo, ln_g, ln_b, out):
    EDGES = edges()
    N_EDGES = We.shape[0]
    A_COLS = 3 * D + 3
    O_COLS = 2 * D + 1
    SETS = 2 + NODES

    def dram(name, shape, dt=F32):
        return nc.dram_tensor(name, shape, dt).ap()

    set_a = dram("set_a", [SETS, D, A_COLS])
    set_v = dram("set_v", [SETS, D, D])
    set_o = dram("set_o", [SETS, D, O_COLS])
    xt = dram("xt", [4 + 4 * NODES, D, S])
    resid = dram("resid", [2 * STEPS, D, S])
    x1_tok = dram("x1_tok", [B, 128, NB, D])
    parts_k = dram("parts_k", [2, 3, HEADS, DH, S], BF16)
    parts_q = dram("parts_q", [2, 3, HEADS, DH, S], BF16)
    dens = dram("dens", [2 * GROUP, S])
    rdens = dram("rdens", [2 * GROUP, S])
    mrows = dram("mrows", [2, 3, GROUP, S], BF16)

    with ExitStack() as ctx:
        def sb(name, shape, dt=F32):
            return ctx.enter_context(nc.sbuf_tensor(name, shape, dt))

        def psum(name, shape):
            return ctx.enter_context(nc.psum_tensor(name, shape, F32))

        def sem(name):
            return ctx.enter_context(nc.semaphore(name))

        k_aug = sb("k_aug", [128, 2, HEADS, S], BF16)
        q_aug = sb("q_aug", [128, 2, HEADS, S], BF16)
        probs = sb("probs", [128, PRING, GROUP, 512])
        v_sb = sb("v_sb", [128, 2, NB, HEADS, 32])
        xk = sb("xk", [128, S])
        xq = sb("xq", [128, S])
        xv = sb("xv", [128, S])
        w_a = sb("w_a", [128, A_COLS])
        w_v = sb("w_v", [128, D])
        w_o = sb("w_o", [128, O_COLS])
        q1 = sb("q1", [128, S])
        k32 = sb("k32", [128, S])
        q32 = sb("q32", [128, S])
        rest = sb("rest", [128, S])
        ksp = sb("ksp", [128, 3, S], BF16)
        qsp = sb("qsp", [128, 3, S], BF16)
        mx = sb("mx", [128, 2, NB, GROUP])
        mrest = sb("mrest", [128, 2, NB, GROUP])
        msp = sb("msp", [128, 2, NB, 3, GROUP], BF16)
        mrow_sb = sb("mrow_sb", [3 * GROUP, 2, S], BF16)
        ctx_t = sb("ctx_t", [128, 2, 2, S])
        den = sb("den", [128, 2 * GROUP * S // 128])
        rden = sb("rden", [128, 2 * GROUP * S // 128])
        rden_b = sb("rden_b", [128, 2, S])
        res_sb = sb("res_sb", [128, S])
        node_t = sb("node_t", [128, S])
        xtok = sb("xtok", [128, NB, D])
        xhat = sb("xhat", [128, NB, D])
        stats = sb("stats", [128, NB, 6])
        mv = sb("mv", [128, NB, 2])
        var = sb("var", [128, NB])
        rest_t = sb("rest_t", [128, S])
        sd = sb("sd", [128, NB])
        rstd = sb("rstd", [128, NB])
        ident = sb("ident", [128, 128])
        identb = sb("identb", [128, 128], BF16)
        gain = sb("gain", [128, D])
        shift = sb("shift", [128, D])

        sc = psum("sc", [128, 3, 512])
        ring = psum("ring", [128, 2, 2, 512])
        acc = psum("acc", [128, 512])

        raw = probs[:, :, :, :].rearrange("p a b c -> p (a b c)")[:, 0:(4 + N_EDGES + 4 * NODES) * D].rearrange(
            "p (m d) -> p m d", d=D)

        def we_raw(c, w):
            return raw[:, 4 + EDGES[c][w], :]

        def w_raw(c, w):
            return raw[:, 4 + N_EDGES + NODES * w + c, :]
        prep = v_sb[:, :, :, :, :].rearrange("p a b c d -> p (a b c d)")
        half_q = q_aug[:, 1, :, :].rearrange("p a b -> p (a b)").bitcast(F32)
        half_k = k_aug[:, 1, :, :].rearrange("p a b -> p (a b)").bitcast(F32)
        st_a = half_q[:, 0:SETS * A_COLS].rearrange("p (s c) -> p s c", s=SETS)
        st_o = half_q[:, SETS * A_COLS:SETS * A_COLS + 2 * O_COLS].rearrange("p (s c) -> p s c", s=2)
        st_v = half_k[:, 0:SETS * D].rearrange("p (s c) -> p s c", s=SETS)
        st_z = half_k[:, SETS * D:SETS * D + NODES * O_COLS].rearrange("p (s c) -> p s c", s=NODES)
        x_in = [ctx_t[:, b // 2, b % 2, :].rearrange("p (k d) -> p k d", k=NB) for b in range(B)]
        x_out = [rden_b[:, 0, :], rden_b[:, 1, :], node_t[:, :], rest_t[:, :]]
        at_we, at_wo, at_woc, at_small, at_rows, at_brow, at_be = 0, 1536, 1664, 2176, 2304, 3072, 3584
        we_t = prep[:, at_we:at_we + 2 * NODES * D].rearrange("p (c w d) -> p c w d", w=2, d=D)
        wo_t = prep[:, at_wo:at_wo + D]
        wo_c = prep[:, at_woc:at_woc + 4 * D].rearrange("p (t j e) -> p t j e", t=4, j=4)
        small = prep[:, at_small:at_small + 64]
        ew_b, aw_b = small[:, 0:3 * NODES], small[:, 18:18 + NODES]
        bes = small[:, 24:24 + 2 * NODES]
        vb = small[:, 36:36 + NODES]
        bvo = small[:, 42:44]
        ones2 = small[:, 44:46]
        ones_col, one = ones2[:, 0:1], ones2[0:1, 0:1]
        rows = prep[0:1, at_rows:at_rows + NODES * D]
        brow = prep[0:1, at_brow:at_brow + 4 * D].rearrange("p (w h c) -> p w h c", w=2, h=2)
        be_rows = prep[0:20, at_be:at_be + D]

        names = """prep_in1 prep_in2 prep_x_stored prep_ln prep_jobs prep_evac prep_made prep_stored prep_zero prep_ones prep_zeroed prep_cleared
            prep_id prep_x prep_norm prep_step ones_set consts
            scores_ready exp_done pv_done acc_ready acc_free ring_full ring_free0 ring_free1
            k_split q_split m_split k_step q_step m_step pool_tick dve_tick sp_tick
            mrow_dram mrow_loaded0 mrow_loaded1 parts_stored aug_loaded0 aug_loaded1
            den_stored den_loaded rden_done rden_stored rden_loaded ctx_done ctx_step q1_stored node_stored loaded x1_loaded
            tok_stored tok_step var_ready sd_done rstd_done xhat_done xt_stored final_step final_stored""".split()
        s = {n: sem(n) for n in names}
        ring_free = [s["ring_free0"], s["ring_free1"]]
        aug_loaded = [s["aug_loaded0"], s["aug_loaded1"]]
        mrow_loaded = [s["mrow_loaded0"], s["mrow_loaded1"]]
        block = ctx.enter_context(nc.Block())

        def ring_use(g, use):
            at = ring_uses(g).index(use)
            return at, (TOTAL[g]["ring"] + at) % 2

        def claim(pe, g, pair, use):
            at, r = ring_use(g, use)
            n = TOTAL[g]["ring"] + at
            v = n // 2
            if pair is not None:
                v = v + (TOTAL[g + 2]["ring"] - TOTAL[g]["ring"]) // 2 * pair
            wait(pe, ring_free[r], v)
            return ring[:, r]

        def filled(eng, g, pair, use):
            at, r = ring_use(g, use)
            eng.wait_ge(s["ring_full"], value("ring", g, pair, at + 1))
            return ring[:, r], ring_free[r]

        def evacuated(eng, g, pair, use):
            at, r = ring_use(g, use)
            v = (TOTAL[g]["ring"] + at) // 2 + 1
            if pair is not None:
                v = v + (TOTAL[g + 2]["ring"] - TOTAL[g]["ring"]) // 2 * pair
            eng.wait_ge(ring_free[r], v)
            if eng.engine == mybir.EngineType.SP and pair is not None:
                eng.sem_inc(s["sp_tick"], 1)

        def evacuated_before(eng, g, pair):
            n = TOTAL[g]["ring"] - 1
            v = n // 2 + 1
            if pair is not None:
                v = v + (TOTAL[g + 2]["ring"] - TOTAL[g]["ring"]) // 2 * pair
            eng.wait_ge(ring_free[n % 2], v)

        def flat(region):
            return region.rearrange("p a b -> p (a b)")

        JOBS = [("wt", w) for w in range(3)] + [("bcol", 0), ("x_t", 0), ("xhat_t", 0)]
        FIRST_JOBS = len(JOBS)
        JOBS += [("x_t", 1), ("xhat_t", 1), ("wo_t", 0), ("be", 0)]
        JOBS += [(kind, c) for c in range(NODES) for kind in ("wek_t", "wev_t")] + [("bo", 0)]
        JOBS += [("cols", c) for c in range(NODES)] + [("wo_c", t) for t in (0, 1, 3, 2)]
        JOBS += [(kind, c) for c in range(NODES) for kind in ("wkk", "wvv", "row")]
        JOBS += [(kind, b) for b in (2, 3) for kind in ("x_t", "xhat_t")]
        job_at = {j: n for n, j in enumerate(JOBS)}

        def job_banks(n):
            return {2 * (n % 2), 2 * (n % 2) + 1} if JOBS[n][0] in ("x_t", "xhat_t") else {n % 4}

        def job_place(n):
            bank = min(job_banks(n))
            return ring[:, bank // 2], ring[:, bank // 2, bank % 2, 0:D]

        def job_after(n):
            kind, i = JOBS[n]
            reads = {"bo": ("wo_t", 0), "wkk": ("wek_t", i), "wvv": ("wev_t", i), "cols": ("be", 0), "row": ("cols", i)}
            if kind == "wo_c" and i == 2:
                reads["wo_c"] = ("bo", 0)
            before = [m for m in range(n) if job_banks(m) & job_banks(n)]
            if kind in reads:
                before.append(job_at[reads[kind]])
            return max(before, default=-1) + 1

        N_IN1 = 3 + 4
        N_IN2 = 1 + 7 + 5
        N_STORED1 = 6
        N_STORED = 2 * B + 2 + 3 + 3 * NODES

        @block.sync
        def _(sp):
            def load(dst, src, part):
                sp.dma_start(dst, src).then_inc(s[f"prep_in{part}"], 16)

            def x_store(b, what):
                sp.wait_ge(s["prep_evac"], job_at[what, b] + 1)
                dst, m = (resid[2 * b], 2 * b) if what == "x_t" else (xt[b], 2 * b + 1)
                sp.dma_start(dst, x_out[m % 4]).then_inc(s["prep_x_stored"], 16)

            for b in range(B):
                sp.dma_start(x_in[b], x[b].rearrange("(k p) d -> p k d", p=128)).then_inc(s["prep_x"], 16)
                if b == 0:
                    for n, w in enumerate((Wq, Wk, Wv)):
                        load(raw[:, n, :], w, 1)
                    sp.wait_ge(s["prep_zero"], 1)
                    for w, bias in enumerate((bq, bk)):
                        for h in range(2):
                            load(brow[:, w, h, :].rearrange("p (a e) -> p a e", e=DH)[:, :, 0:8],
                                 bias[64 * h:64 * h + 64].rearrange("(o a e) -> o a e", o=1, e=8), 1)
            x_store(0, "x_t")
            x_store(0, "xhat_t")
            for h in range(2):
                sp.dma_start(set_a[h], st_a[:, h, :]).then_inc(s["prep_x_stored"], 16)
                sp.dma_start(set_v[h], st_v[:, h, :]).then_inc(s["prep_x_stored"], 16)
            sp.wait_ge(s["prep_x_stored"], 16 * N_STORED1)

            def second_part():
                x_store(1, "x_t")
                x_store(1, "xhat_t")
                sp.wait_ge(s["prep_cleared"], 2)
                for c in range(NODES):
                    sp.wait_ge(s["prep_step"], 3)
                    sp.dma_start(set_o[2 + c], st_z[:, c, :]).then_inc(s["prep_zeroed"], 16)
                sp.wait_ge(s["prep_evac"], job_at["row", NODES - 1] + 1)
                sp.dma_start(set_a[2:].rearrange("s p c -> p s c"), st_a[:, 2:, :]).then_inc(s["prep_stored"], 16)
                sp.dma_start(set_v[2:].rearrange("s p c -> p s c"), st_v[:, 2:, :]).then_inc(s["prep_stored"], 16)
                sp.dma_start(set_o[0:2].rearrange("s p c -> p s c"), st_o).then_inc(s["prep_stored"], 16)
                sp.wait_ge(s["prep_zeroed"], 16 * NODES)
                for c in range(NODES):
                    for hg in range(2):
                        sp.dma_start(set_o[2 + c, :, hg * D:hg * D + D].rearrange("(j e) o -> j e o", e=32)[:, 0:DH, :],
                                     fWo[c][64 * hg:64 * hg + 64, :].rearrange("(j d) o -> j d o", j=4)).then_inc(s["prep_stored"], 16)
                    sp.dma_start(set_o[2 + c, DH:DH + 1, 0:D], rows[:, c * D:(c + 1) * D]).then_inc(s["prep_stored"], 16)
                for b in (2, 3):
                    x_store(b, "x_t")
                    x_store(b, "xhat_t")
                sp.wait_ge(s["prep_stored"], 16 * (3 + 3 * NODES))
                sp.wait_ge(s["prep_x_stored"], 16 * (N_STORED1 + 6))

            def hold(eng, sem_, v):
                wait(eng, sem_, v)
                if not isinstance(v, int):
                    eng.sem_inc(s["sp_tick"], 1)

            def weight_set(step):
                if isinstance(step, int):
                    return step % 2 if step < ATTN_STEPS else 2 + (step - ATTN_STEPS) // B
                return (step - ATTN_STEPS) // B + 2

            def source(step, which):
                if isinstance(step, int) and step < ATTN_STEPS:
                    return step // 2
                t = step - ATTN_STEPS
                c, b = t // B, t % B
                if which == "q":
                    return t + 4
                if which == "k":
                    return (c + 3) // 8 * 4 + b + 4
                return (c + 1) // 2 * 4 + b + 4

            def loads_for(g, pair):
                if has_proj(g):
                    st = g + 2 if pair is None else pair * 2 + (g + 2)
                    sp.dma_start(xk[:, :], xt[source(st, "k")]).then_inc(s["loaded"], 16)
                    sp.dma_start(xq[:, :], xt[source(st, "q")]).then_inc(s["loaded"], 16)
                    sp.dma_start(w_a[:, :], set_a[weight_set(st)]).then_inc(s["loaded"], 16)
                if has_max(g):
                    st = g + 1 if pair is None else pair * 2 + (g + 1)
                    sp.dma_start(xv[:, :], xt[source(st, "v")]).then_inc(s["loaded"], 16)
                    sp.dma_start(w_v[:, :], set_v[weight_set(st)]).then_inc(s["loaded"], 16)
                if has_out(g):
                    st = g - 1 if pair is None else pair * 2 + (g - 1)
                    sp.dma_start(w_o[:, :], set_o[weight_set(st)]).then_inc(s["loaded"], 16)
                    at = st if g - 1 < ATTN_STEPS else st + STEPS
                    sp.dma_start(res_sb[:, :], resid[at]).then_inc(s["loaded"], 16)

            def aug_loads(g, hg):
                par = g % 2
                heads = slice(GROUP * hg, GROUP * hg + GROUP)
                src_k = parts_k[par][:, heads].rearrange("a h d t -> a d h t")
                src_q = parts_q[par][:, heads].rearrange("a h d t -> a d h t")
                for t, (pk, pq) in enumerate([(0, 0), (0, 1), (0, 2), (1, 0), (1, 1), (2, 0)]):
                    sp.dma_start(k_aug[DH * t:DH * t + DH, par, heads, :], src_k[pk]).then_inc(aug_loaded[hg], 16)
                    sp.dma_start(q_aug[DH * t:DH * t + DH, par, heads, :], src_q[pq]).then_inc(aug_loaded[hg], 16)

            def mrow_move(g, pair, hg, par, done, before):
                evacuated(sp, g, pair, ("mrow", hg))
                hold(sp, mrow_loaded[hg], before)
                sp.dma_start(mrows[hg].rearrange("a h t -> (a h) t"), mrow_sb[:, hg, :]).then_inc(s["mrow_dram"], 16)
                hold(sp, s["mrow_dram"], done * 16)
                sp.dma_start(q_aug[KR:KM, par, GROUP * hg:GROUP * hg + GROUP, :], mrows[hg]).then_inc(mrow_loaded[hg], 16)

            def mrow_loads(g, pair, hg):
                v = 16 * (g if hg else g + 1)
                return v if pair is None else pair * 32 + v

            def body(g, pair):
                par = g % 2
                if tail(g) == "last":
                    hold(sp, s["final_step"], value("last", g, pair, 0, 3))
                    sp.dma_start(res_tok, x1_tok[(g - 1) % B]).then_inc(s["x1_loaded"], 16)
                if has_out(g):
                    hold(sp, s["acc_free"], value("acc", g, pair, 1))
                    for hg in range(2):
                        for j in range(GROUP):
                            sp.dma_start(dens[GROUP * hg + j:GROUP * hg + j + 1, :],
                                         ctx_t[32 * j + DH:32 * j + DH + 1, 1 - par, hg, :]).then_inc(s["den_stored"], 16)
                    hold(sp, s["den_stored"], value("out", g, pair, 16 * 8, 16 * 8))
                    sp.dma_start(den[:, :], dens.rearrange("h (a t) -> (h a) t", a=16)).then_inc(s["den_loaded"], 16)
                if has_b(g):
                    mrow_move(g, pair, 1, par, value("mrow", g, pair, 1), mrow_loads(g, pair, 1))
                if has_out(g):
                    hold(sp, s["rden_done"], value("out", g, pair, 1))
                    sp.dma_start(rdens.rearrange("h (a t) -> (h a) t", a=16), rden[:, :]).then_inc(s["rden_stored"], 16)
                    hold(sp, s["rden_stored"], value("out", g, pair, 16, 16))
                    for j in range(GROUP):
                        src = rdens.rearrange("(g h) t -> h g t", g=2)[j:j + 1]
                        sp.dma_start(rden_b[32 * j:32 * j + 32, :, :], src.broadcast_to([32, 2, S])).then_inc(s["rden_loaded"], 16)
                if has_proj(g):
                    st = g + 2 if pair is None else pair * 2 + (g + 2)
                    evacuated(sp, g, pair, ("q1", 0))
                    sp.dma_start(resid[st + STEPS], q1[:, :]).then_inc(s["q1_stored"], 16)
                    hold(sp, s["k_split"], value("proj", g, pair, 1))
                    sp.dma_start(parts_k[par].rearrange("a h d t -> (h d) a t"), ksp[:, :, :]).then_inc(s["parts_stored"], 16)
                    hold(sp, s["q_split"], value("proj", g, pair, 1))
                    sp.dma_start(parts_q[par].rearrange("a h d t -> (h d) a t"), qsp[:, :, :]).then_inc(s["parts_stored"], 16)
                if has_out(g):
                    evacuated(sp, g, pair, ("out", 0))
                    st = g - 1 if pair is None else pair * 2 + (g - 1)
                    if tail(g) == "":
                        if g - 1 < ATTN_STEPS:
                            sp.dma_start(resid[st + 1], node_t[:, :]).then_inc(s["node_stored"], 16)
                        else:
                            sp.dma_start(xt[st], node_t[:, :]).then_inc(s["node_stored"], 16)
                if has_proj(g):
                    hold(sp, s["parts_stored"], value("proj", g, pair, 32, 32))
                    if has_b(g):
                        hold(sp, s["scores_ready"], value("scores", g, pair, 64))
                    aug_loads(g, 0)
                if has_max(g):
                    mrow_move(g, pair, 0, 1 - par, value("mrow", g, pair, 1 + has_b(g)), mrow_loads(g, pair, 0))
                if tail(g):
                    b = (g - 1) // 2 if pair is None else pair + (g - 1) // 2
                    if tail(g) == "mid":
                        evacuated(sp, g, pair, ("t1", 0))
                        sp.dma_start(x1_tok[b], xtok[:, :, :]).then_inc(s["tok_stored"], 16)
                        evacuated(sp, g, pair, ("t2", 0))
                        sp.dma_start(xt[b + 4], rest2).then_inc(s["xt_stored"], 16)
                    else:
                        hold(sp, s["final_step"], value("last", g, pair, 3, 3))
                        sp.dma_start(out[(g - 1) % B].rearrange("(k p) d -> p k d", p=128), xhat[:, :, :]).then_inc(s["final_stored"], 16)
                if g == G0:
                    aug_loads(g, 1)
                if g < STEPS:
                    n = g + 1
                    if has_proj(g):
                        evacuated(sp, g, pair, ("q", 0))
                        hold(sp, s["q1_stored"], value("proj", g, pair, 16, 16))
                    if has_max(g):
                        evacuated(sp, g, pair, ("v", 0))
                    if has_out(g):
                        evacuated(sp, g, pair, ("out", 0))
                    if has_out(g) and tail(g) == "":
                        hold(sp, s["node_stored"], node_value(g, pair))
                    if tail(g) == "mid":
                        hold(sp, s["xt_stored"], value("mid", g, pair, 16, 16))
                        hold(sp, s["tok_stored"], value("mid", g, pair, 16, 16))
                    loads_for(n, pair)
                    if g == G0:
                        second_part()
                if has_proj(g) and g > G0:
                    if has_b(g):
                        hold(sp, s["scores_ready"], value("scores", g, pair, 128))
                    aug_loads(g, 1)

            def node_value(g, pair):
                n = sum(1 for i in range(G0, g + 1) if has_out(i) and tail(i) == "")
                if pair is None:
                    return 16 * n
                per = sum(1 for i in (g + 1, g + 2) if has_out(i) and tail(i) == "")
                return 16 * n + 16 * per * pair

            rest2 = rest_t[:, :]
            res_tok = rest_t[:, :].rearrange("p (k d) -> p k d", k=NB)
            loads_for(G0, None)
            load(raw[:, 3, :], Wo, 2)
            load(be_rows, be, 2)
            load(bvo[:, 0:1], bv.rearrange("(d o) -> d o", o=1), 2)
            load(bvo[:, 1:2], bo.rearrange("(d o) -> d o", o=1), 2)
            load(ew_b, ew.rearrange("(o c) w -> o (c w)", o=1).partition_broadcast(128), 2)
            load(aw_b, act_w.rearrange("(o c) -> o c", o=1).partition_broadcast(128), 2)
            load(gain[:, :], ln_g.rearrange("(o c) -> o c", o=1).partition_broadcast(128), 2)
            load(shift[:, :], ln_b.rearrange("(o c) -> o c", o=1).partition_broadcast(128), 2)
            load(raw[:, 4:4 + N_EDGES, :], We.rearrange("e p d -> p e d"), 2)
            for n, w in enumerate((fWq, fWk, fWv, fWo)):
                at = 4 + N_EDGES + NODES * n
                load(raw[:, at:at + NODES, :], w.rearrange("c p d -> p c d"), 2)
            for g in range(G0, LOOPS[1][0]):
                body(g, None)
            iterations(sp, body, LOOPS[1][0])
            hold(sp, s["final_stored"], 16 * B)
            hold(sp, s["node_stored"], node_value(STEPS, None))
            hold(sp, s["mrow_dram"], value("mrow", STEPS, None, 0, 16))

        @block.tensor
        def _(pe):
            def jobs(first, last_job):
                for n in range(first, last_job):
                    kind, i = JOBS[n]
                    region, out1 = job_place(n)
                    wait(pe, s["prep_evac"], job_after(n))
                    if kind == "be":
                        last = pe.transpose(out1[:, 0:20], be_rows, ident[0:20, 0:20])
                    elif kind == "wt":
                        last = pe.transpose(out1, raw[:, i, :], ident[:, :])
                    elif kind == "bcol":
                        for w in range(2):
                            for h in range(2):
                                last = pe.matmul(out1[:, 2 * w + h:2 * w + h + 1], brow[:, w, h, :], one, start=True, stop=True)
                    elif kind == "wo_t":
                        last = pe.transpose(out1, raw[:, 3, :], ident[:, :])
                    elif kind == "bo":
                        last = pe.matmul(out1[:, 0:1], wo_t, bvo[:, 0:1], start=True, stop=True)
                    elif kind == "wo_c":
                        pe.wait_ge(s["prep_step"], 2)
                        last = pe.transpose(out1, wo_c[:, i].rearrange("p j e -> p (j e)"), ident[:, :])
                    elif kind in ("wek_t", "wev_t"):
                        last = pe.transpose(out1, we_raw(i, 1 if kind == "wek_t" else 2), ident[:, :])
                    elif kind in ("wkk", "wvv"):
                        w = 0 if kind == "wkk" else 1
                        last = pe.matmul(out1, we_t[:, i, w], w_raw(i, 1 + w), start=True, stop=True)
                    elif kind == "cols":
                        pe.matmul(out1[:, 0:1], w_raw(i, 1), bes[:, 2 * i:2 * i + 1], start=True, stop=True)
                        last = pe.matmul(out1[:, 1:2], w_raw(i, 2), bes[:, 2 * i + 1:2 * i + 2], start=True, stop=True)
                    elif kind == "row":
                        last = pe.matmul(out1[0:1, :], vb[:, i:i + 1], w_raw(i, 3), start=True, stop=True)
                    else:
                        if kind == "x_t":
                            pe.wait_ge(s["prep_x"], 16 * (i + 1))
                        else:
                            pe.wait_ge(s["prep_norm"], i + 1)
                        src = x_in[i] if kind == "x_t" else xhat
                        for k in range(NB):
                            last = pe.transpose(region[:, k // 4, 128 * (k % 4):128 * (k % 4) + 128], src[:, k, :], ident[:, :])
                    last.then_inc(s["prep_jobs"], 1)

            def project(g, pair, use, w, src, ready=None):
                region = claim(pe, g, pair, use)
                for half in range(2):
                    last = pe.matmul(region[:, half, :], w, src[:, 512 * half:512 * half + 512], start=True, stop=True)
                last.then_inc(s["ring_full"], 1)

            def chore(g, pair, use):
                kind, hg = use
                if kind == "k":
                    pe.wait_ge(s["loaded"], value("loads", g + 1, pair))
                    project(g, pair, use, w_a[:, 2 * D:3 * D], xk)
                elif kind == "q1":
                    project(g, pair, use, w_a[:, 0:D], xq)
                elif kind == "q":
                    evacuated(pe, g, pair, ("q1", 0))
                    project(g, pair, use, w_a[:, D:2 * D], q1)
                elif kind == "v":
                    pe.wait_ge(s["loaded"], value("loads", g + 1, pair))
                    region = claim(pe, g, pair, use)
                    for k in range(NB):
                        last = pe.matmul(region[:, k // 4, 128 * (k % 4):128 * (k % 4) + 128],
                                         xv[:, 128 * k:128 * k + 128], w_v[:, :], start=True, stop=True)
                    last.then_inc(s["ring_full"], 1)
                elif kind == "mrow":
                    done = value("mrow", g, pair, 1 if hg else 1 + has_b(g))
                    pe.wait_ge(s["m_split"], done)
                    region = claim(pe, g, pair, use)
                    for k in range(NB):
                        last = pe.matmul(region[0:3 * GROUP, k // 4, 128 * (k % 4):128 * (k % 4) + 128],
                                         msp[:, hg, k].rearrange("p a h -> p (a h)"), identb[:, :], start=True, stop=True)
                    last.then_inc(s["ring_full"], 1)
                elif kind == "out":
                    pe.wait_ge(s["loaded"], value("loads", g + 1, pair))
                    pe.wait_ge(s["ctx_done"], value("out", g, pair, 1))
                    region = claim(pe, g, pair, use)
                    for half in range(2):
                        for hg2 in range(2):
                            last = pe.matmul(region[:, half, :], w_o[:, D * hg2:D * hg2 + D],
                                             ctx_t[:, (g - 1) % 2, hg2, 512 * half:512 * half + 512], start=hg2 == 0, stop=hg2 == 1)
                    last.then_inc(s["ring_full"], 1)
                else:
                    if kind == "t1":
                        evacuated(pe, g, pair, ("out", 0))
                    else:
                        pe.wait_ge(s["xhat_done"], value("tail", g, pair, 1))
                    region = claim(pe, g, pair, use)
                    for k in range(NB):
                        src = node_t[:, 128 * k:128 * k + 128] if kind == "t1" else xhat[:, k, :]
                        last = pe.transpose(region[:, k // 4, 128 * (k % 4):128 * (k % 4) + 128], src, ident[:, :])
                    last.then_inc(s["ring_full"], 1)

            def score(g, pair, n, j):
                i = 4 * n + j
                before = i - 2 if i >= 3 else (-1, 0, -2)[i]
                wait(pe, s["exp_done"], value("scores", g, pair, before))
                hg, qh, kc = n // 16, n // 8 % 2, n % 8
                h = GROUP * hg + j
                pe.matmul(sc[:, i % 3, :], k_aug[0:KM, g % 2, h, 128 * kc:128 * kc + 128],
                          q_aug[0:KM, g % 2, h, 512 * qh:512 * qh + 512], start=True, stop=True).then_inc(s["scores_ready"], 1)

            def max_scores(g, pair, u):
                hg, qb, h = u // 32, u % 32 // 4, u // 32 * GROUP + u % 4
                region = claim(pe, g, pair, ("max", u))
                par = (g + 1) % 2
                for half in range(2):
                    last = pe.matmul(region[:, half, :], q_aug[0:KR, par, h, 128 * qb:128 * qb + 128],
                                     k_aug[0:KR, par, h, 512 * half:512 * half + 512], start=True, stop=True)
                last.then_inc(s["ring_full"], 1)

            def pv(g, pair, t):
                par, t_in = (g % 2, t) if t >= 0 else ((g - 1) % 2, t + SLOTS)
                hg, kc = t_in // 16, t_in % 8
                pe.wait_ge(s["exp_done"], value("scores", g, pair, 4 * (t + 1)))
                if kc == 0:
                    wait(pe, s["acc_free"], value("acc", g, pair, t_in // 8 + has_out(g)))
                for j in range(GROUP):
                    last = pe.matmul(acc[32 * j:32 * j + 32, :], v_sb[:, par, kc, GROUP * hg + j, :],
                                     probs[:, t_in % PRING, j, :], start=kc == 0, stop=kc == 7)
                last.then_inc(s["pv_done"], 1)

            def body(g, pair):
                for n in range(SLOTS):
                    if has_max(g) and n % 16 == 0:
                        pe.wait_ge(aug_loaded[n // 16], aug_value(g, pair))
                    if has_b(g) and n % 16 == 0:
                        pe.wait_ge(mrow_loaded[n // 16], mrow_value(g, pair))
                    for half in range(2):
                        if half:
                            for use in chores(g, n):
                                chore(g, pair, use)
                        if has_b(g):
                            score(g, pair, n, 2 * half)
                            score(g, pair, n, 2 * half + 1)
                        if has_max(g):
                            max_scores(g, pair, 2 * n + half)
                    for t in pv_slots(g, n):
                        pv(g, pair, t)

            def aug_value(g, pair):
                v = 16 * 2 * TERMS * (g + 2)
                return v if pair is None else v + 16 * 2 * TERMS * 2 * pair

            def mrow_value(g, pair):
                return 16 * (g + 1) if pair is None else pair * 32 + 16 * (g + 1)

            pe.wait_ge(s["prep_id"], 3)
            pe.wait_ge(s["prep_in1"], 16 * N_IN1)
            pe.wait_ge(s["prep_step"], 1)
            jobs(0, FIRST_JOBS)
            pe.wait_ge(s["prep_evac"], FIRST_JOBS)
            body(G0, None)
            pe.wait_ge(s["prep_in2"], 16 * N_IN2)
            evacuated(pe, G0, None, ("q1", 0))
            evacuated(pe, G0, None, ("q", 0))
            jobs(FIRST_JOBS, len(JOBS))
            pe.wait_ge(s["prep_evac"], len(JOBS))
            body(G0 + 1, None)
            pe.wait_ge(s["consts"], 2)
            pe.wait_ge(s["ones_set"], 2)
            iterations(pe, body, G0 + 2)

        @block.scalar
        def _(act):
            def deviation(b):
                act.wait_ge(s["var_ready"], b + 1)
                act.activation(sd[:, :], var[:, :], ACT.Sqrt).then_inc(s["sd_done"], 1)

            def chore(g, pair, use):
                if use[0] == "t2":
                    region, free = filled(act, g, pair, use)
                    act.activation(rest_t[:, :], flat(region), ACT.Copy).then_inc(free, 1)

            def body(g, pair):
                for n in range(SLOTS):
                    for use in chores(g, n):
                        chore(g, pair, use)
                    if has_b(g):
                        if n >= PRING or has_out(g):
                            act.wait_ge(s["pv_done"], value("pv", g, pair, n - PRING + 1 + 2 * has_out(g)))
                        for j in range(GROUP):
                            if j == 1:
                                contexts(g, pair, n)
                            i = 4 * n + j
                            act.wait_ge(s["scores_ready"], value("scores", g, pair, i + 1))
                            act.activation(probs[:, n % PRING, j, :], sc[:, i % 3, :], ACT.Exp).then_inc(s["exp_done"], 1)
                    else:
                        contexts(g, pair, n)
                    if tail(g) and n == AT_T1 + 6:
                        act.wait_ge(s["var_ready"], value("tail", g, pair, B + 1))
                        act.activation(sd[:, :], var[:, :], ACT.Sqrt).then_inc(s["sd_done"], 1)

            def contexts(g, pair, n):
                if n == AT_DEN and has_out(g):
                    context(g, pair, (g - 1) % 2, 3, 2)
                if n in (10, 18, 26) and has_b(g):
                    q = n // 8 - 1
                    context(g, pair, g % 2, q, 8 * (q + 1) + 2 * has_out(g))

            def context(g, pair, par, q, pvs):
                act.wait_ge(s["pv_done"], value("pv", g, pair, pvs))
                act.activation(ctx_t[:, par, q // 2, 512 * (q % 2):512 * (q % 2) + 512], acc[:, :],
                               ACT.Copy).then_inc(s["acc_free"], 1)

            deviation(0)
            body(G0, None)
            for b in range(1, B):
                deviation(b)
            act.wait_ge(s["prep_evac"], len(JOBS))
            act.wait_ge(s["prep_stored"], 16 * (3 + 3 * NODES))
            act.wait_ge(s["prep_x_stored"], 16 * (N_STORED1 + 6))
            iterations(act, body, G0 + 1)

        @block.gpsimd
        def _(pool):
            pool.memset(ident[:, :], 0.0).then_inc(s["prep_id"], 1)
            pool.wait_ge(s["prep_id"], 1)
            pool.affine_select(out=ident[:, :], in_=ident[:, :], compare_op=ALU.not_equal, fill=1.0, base=0,
                               pattern=[[-1, 128]], channel_multiplier=1).then_inc(s["prep_id"], 1)
            pool.wait_ge(s["prep_id"], 2)
            pool.tensor_copy(identb[:, :], ident[:, :]).then_inc(s["prep_id"], 1)
            pool.wait_ge(s["prep_id"], 3)
            pool.memset(k_aug[KR:KM, 0, :, :], -1.0).then_inc(s["consts"], 1)
            pool.wait_ge(s["consts"], 1)

            def split(src, parts, tmp, step, first, done):
                pool.sem_inc(s["pool_tick"], 1)
                pool.tensor_copy(parts[0], src).then_inc(step, 1)
                pool.wait_ge(step, first + 1)
                pool.tensor_tensor(tmp, src, parts[0], ALU.subtract).then_inc(step, 1)
                pool.wait_ge(step, first + 2)
                pool.sem_inc(s["pool_tick"], 1)
                pool.tensor_copy(parts[1], tmp).then_inc(step, 1)
                pool.wait_ge(step, first + 3)
                pool.tensor_tensor(parts[2], tmp, parts[1], ALU.subtract).then_inc(done, 1)

            def m_split(g, pair, hg, nth):
                if hg:
                    evacuated_before(pool, g, pair)
                else:
                    evacuated(pool, g, pair, ("max", 31))
                split(mx[:, hg], [msp[:, hg, :, a, :] for a in range(3)], mrest[:, hg], s["m_step"],
                      value("mrow", g, pair, 3 * nth, 3), s["m_split"])

            def context(g, pair):
                wait(pool, s["k_split"], value("proj", g, pair, int(has_proj(g))))
                pool.wait_ge(s["rden_loaded"], value("out", g, pair, 16 * GROUP, 16 * GROUP))
                part = ctx_t[:, (g - 1) % 2, :, :]
                pool.tensor_tensor(part, part, rden_b[:, :, :], ALU.mult).then_inc(s["ctx_done"], 1)

            def body(g, pair):
                if has_b(g):
                    m_split(g, pair, 1, 0)
                if has_proj(g):
                    for use, src, parts, step, done in (("k", k32, ksp, "k_step", "k_split"), ("q", q32, qsp, "q_step", "q_split")):
                        evacuated(pool, g, pair, (use, 0))
                        if g > G0:
                            pool.wait_ge(s["parts_stored"], value("proj", g, pair, 0, 32))
                        if use == "q":
                            pool.wait_ge(s["k_split"], value("proj", g, pair, 1))
                            if has_out(g):
                                pool.wait_ge(s["ctx_done"], value("out", g, pair, 1))
                        split(src[:, :], [parts[:, a, :] for a in range(3)], rest[:, :], s[step],
                              value("proj", g, pair, 0, 3), s[done])
                        if use == "k" and has_out(g):
                            context(g, pair)
                elif has_out(g):
                    context(g, pair)
                if has_max(g):
                    m_split(g, pair, 0, int(has_b(g)))

            body(G0, None)
            pool.wait_ge(s["q_split"], 1)
            pool.wait_ge(s["prep_evac"], len(JOBS))
            pool.wait_ge(s["prep_stored"], 16 * (3 + 3 * NODES))
            for par in range(2):
                if par:
                    pool.wait_ge(s["ones_set"], 1)
                pool.memset(v_sb[:, par].rearrange("p k h e -> p (k h) e")[:, :, DH:32], 1.0).then_inc(s["ones_set"], 1)
            pool.wait_ge(s["ones_set"], 2)
            pool.memset(k_aug[KR:KM, 1, :, :], -1.0).then_inc(s["consts"], 1)
            pool.wait_ge(s["consts"], 2)
            iterations(pool, body, G0 + 1)

        @block.vector
        def _(dve):
            dve.memset(prep[:, :], 0.0).then_inc(s["prep_zero"], 1)
            dve.memset(st_a[:, :, :], 0.0).then_inc(s["prep_cleared"], 1)
            dve.memset(half_k[:, 0:SETS * D + NODES * O_COLS], 0.0).then_inc(s["prep_cleared"], 1)
            dve.wait_ge(s["prep_zero"], 1)
            dve.wait_ge(s["prep_cleared"], 2)
            dve.memset(ones2, 1.0).then_inc(s["prep_step"], 1)
            dve.wait_ge(s["prep_id"], 2)
            for h in range(2):
                dve.tensor_copy(st_a[:, h, 0:D], ident[:, :])

            def chore(g, pair, use):
                kind, hg = use
                if kind not in ("k", "q1", "q", "v", "mrow"):
                    return
                region, free = filled(dve, g, pair, use)
                if kind == "v":
                    if g == G0 + 1:
                        dve.wait_ge(s["prep_stored"], 16 * (3 + 3 * NODES))
                    dve.tensor_copy(v_sb[:, (g + 1) % 2].rearrange("p k h e -> p (k h) e")[:, :, 0:DH],
                                    flat(region).rearrange("p (a e) -> p a e", e=DH)).then_inc(free, 1)
                elif kind == "mrow":
                    dve.tensor_copy(mrow_sb[:, hg, :], flat(region)[0:3 * GROUP, :]).then_inc(free, 1)
                else:
                    tile, col = {"q1": (q1, 0), "q": (q32, 1), "k": (k32, 2)}[kind]
                    dve.tensor_scalar(tile[:, :], flat(region), w_a[:, 3 * D + col:3 * D + col + 1], None,
                                      ALU.add).then_inc(free, 1)

            def second_operands():
                dve.wait_ge(s["prep_in2"], 16 * N_IN2)
                dve.wait_ge(s["prep_step"], 1)
                for h in range(2):
                    dve.tensor_copy(st_o[:, h, 2 * D:], ones_col)
                for t in range(4):
                    last = dve.tensor_copy(wo_c[:, t, :, 0:8], raw[:, 3, 32 * t:32 * t + 32].rearrange("p (j e) -> p j e", e=8))
                last.then_inc(s["prep_step"], 1)
                for c in range(NODES):
                    dve.tensor_scalar(st_a[:, 2 + c, 0:D], we_raw(c, 0), ew_b[:, 3 * c:3 * c + 1], None, ALU.mult)
                    dve.tensor_scalar(st_a[:, 2 + c, D:2 * D], w_raw(c, 0), DH ** -0.5, None, ALU.mult)
                    last = dve.tensor_copy(st_z[:, c, 2 * D:], aw_b[:, c:c + 1])
                last.then_inc(s["prep_step"], 1)

            factor = 8 ** -0.5
            for n, (kind, i) in enumerate(JOBS):
                region, out1 = job_place(n)
                if n == FIRST_JOBS:
                    for use in ring_uses(G0):
                        chore(G0, None, use)
                    second_operands()
                if kind == "x_t":
                    dve.wait_ge(s["prep_x"], 16 * (i + 1))
                    for k in range(NB):
                        last = dve.bn_stats(stats[:, k, :], x_in[i][:, k, :])
                    last.then_inc(s["prep_ln"], 1)
                    dve.wait_ge(s["prep_ln"], 1 + 3 * i)
                    for k in range(NB):
                        last = dve.bn_aggr(mv[:, k, :], stats[:, k, :])
                    last.then_inc(s["prep_ln"], 1)
                    dve.wait_ge(s["prep_ln"], 2 + 3 * i)
                    dve.tensor_scalar(var[:, :], mv[:, :, 1], 1e-5, None, ALU.add).then_inc(s["var_ready"], 1)
                    dve.wait_ge(s["sd_done"], i + 1)
                    dve.reciprocal(rstd[:, :], sd[:, :]).then_inc(s["prep_ln"], 1)
                    dve.wait_ge(s["prep_ln"], 3 + 3 * i)
                    for k in range(NB):
                        last = dve.tensor_scalar(xhat[:, k, :], x_in[i][:, k, :], mv[:, k, 0:1], rstd[:, k:k + 1], ALU.subtract, ALU.mult)
                    last.then_inc(s["prep_norm"], 1)
                dve.wait_ge(s["prep_jobs"], n + 1)
                if kind == "be":
                    for c, edge in enumerate(EDGES):
                        for w, dst in ((1, bes[:, 2 * c:2 * c + 1]), (2, bes[:, 2 * c + 1:2 * c + 2]),
                                       (0, st_a[:, 2 + c, 3 * D:3 * D + 1])):
                            e = edge[w]
                            last = dve.tensor_scalar(dst, out1[:, e:e + 1], ew_b[:, 3 * c + w:3 * c + w + 1], None, ALU.mult)
                elif kind == "wt":
                    for h in range(2):
                        src = out1[:, 64 * h:64 * h + 64].rearrange("p (a e) -> p a e", e=8)
                        if i == 2:
                            dst = st_v[:, h, :]
                        else:
                            dst = st_a[:, h, D * (1 + i):D * (2 + i)]
                        last = dve.tensor_scalar(dst.rearrange("p (a e) -> p a e", e=DH)[:, :, 0:8], src,
                                                 factor if i == 0 else 1.0, None, ALU.mult)
                elif kind == "bcol":
                    for w in range(2):
                        for h in range(2):
                            last = dve.tensor_scalar(st_a[:, h, 3 * D + 1 + w:3 * D + 2 + w], out1[:, 2 * w + h:2 * w + h + 1],
                                                     1.0 if w else factor, None, ALU.mult)
                elif kind == "wo_t":
                    last = dve.tensor_copy(wo_t, out1)
                elif kind == "bo":
                    dve.wait_ge(s["prep_step"], 2)
                    last = dve.tensor_tensor(wo_c[:, 2, 0, DH:DH + 1], out1[:, 0:1], bvo[:, 1:2], ALU.add)
                elif kind == "wo_c":
                    last = dve.tensor_copy(st_o[:, i // 2, D * (i % 2):D * (i % 2) + D], out1)
                elif kind == "wek_t":
                    last = dve.tensor_scalar(we_t[:, i, 0], out1, ew_b[:, 3 * i + 1:3 * i + 2], None, ALU.mult)
                elif kind == "wev_t":
                    last = dve.tensor_scalar(we_t[:, i, 1], out1, ew_b[:, 3 * i + 2:3 * i + 3], None, ALU.mult)
                elif kind == "wkk":
                    last = dve.tensor_copy(st_a[:, 2 + i, 2 * D:3 * D], out1)
                elif kind == "wvv":
                    last = dve.tensor_copy(st_v[:, 2 + i, :], out1)
                elif kind == "cols":
                    dve.tensor_copy(st_a[:, 2 + i, 3 * D + 2:3 * D + 3], out1[:, 0:1])
                    last = dve.tensor_copy(vb[:, i:i + 1], out1[:, 1:2])
                elif kind == "row":
                    last = dve.tensor_copy(rows[:, i * D:(i + 1) * D], out1[0:1, :])
                elif kind == "x_t":
                    if i >= 2:
                        dve.wait_ge(s["prep_x_stored"], 16 * (N_STORED1 + 2 * (i - 2)))
                    last = dve.tensor_copy(x_out[2 * i % 4], flat(region))
                else:
                    last = dve.tensor_copy(x_out[(2 * i + 1) % 4], flat(region))
                last.then_inc(s["prep_evac"], 1)

            def tail_part(g, pair, n):
                k0 = n - AT_T1
                if k0 == 0:
                    region, free = filled(dve, g, pair, ("t1", 0))
                    dve.tensor_copy(xtok[:, :, :].rearrange("p k d -> p (k d)"), flat(region)).then_inc(free, 1)
                elif 1 <= k0 <= 4:
                    if k0 == 1:
                        evacuated(dve, g, pair, ("t1", 0))
                    for k in (2 * k0 - 2, 2 * k0 - 1):
                        last = dve.bn_stats(stats[:, k, :], xtok[:, k, :])
                    if k0 == 4:
                        last.then_inc(s["tok_step"], 1)
                elif k0 == 5:
                    dve.wait_ge(s["tok_step"], value("tail", g, pair, 1, 2))
                    dve.sem_inc(s["dve_tick"], 1)
                    for k in range(NB):
                        last = dve.bn_aggr(mv[:, k, :], stats[:, k, :])
                    last.then_inc(s["tok_step"], 1)
                    dve.wait_ge(s["tok_step"], value("tail", g, pair, 2, 2))
                    dve.tensor_scalar(var[:, :], mv[:, :, 1], 1e-5 if tail(g) == "mid" else 1e-6, None,
                                      ALU.add).then_inc(s["var_ready"], 1)
                elif k0 == 8:
                    dve.wait_ge(s["sd_done"], value("tail", g, pair, B + 1))
                    dve.reciprocal(rstd[:, :], sd[:, :]).then_inc(s["rstd_done"], 1)
                    dve.wait_ge(s["rstd_done"], value("tail", g, pair, 1))
                    if tail(g) == "last":
                        wait(dve, s["final_stored"], value("last", g, pair, 0, 16))
                    for k in range(NB):
                        last = dve.tensor_scalar(xhat[:, k, :], xtok[:, k, :], mv[:, k, 0:1], rstd[:, k:k + 1], ALU.subtract, ALU.mult)
                    last.then_inc(s["xhat_done"], 1)
                elif k0 == 10 and tail(g) == "last":
                    dve.wait_ge(s["xhat_done"], value("tail", g, pair, 1))
                    dve.tensor_tensor(xhat[:, :, :], xhat[:, :, :], gain[:, :].rearrange("p (o d) -> p o d", o=1).broadcast_to([128, NB, D]),
                                      ALU.mult).then_inc(s["final_step"], 1)
                    dve.wait_ge(s["final_step"], value("last", g, pair, 1, 3))
                    dve.tensor_tensor(xhat[:, :, :], xhat[:, :, :], shift[:, :].rearrange("p (o d) -> p o d", o=1).broadcast_to([128, NB, D]),
                                      ALU.add).then_inc(s["final_step"], 1)
                    dve.wait_ge(s["final_step"], value("last", g, pair, 2, 3))
                    dve.wait_ge(s["x1_loaded"], value("last", g, pair, 16, 16))
                    dve.tensor_tensor(xhat[:, :, :], xhat[:, :, :], rest_t[:, :].rearrange("p (k d) -> p k d", k=NB),
                                      ALU.add).then_inc(s["final_step"], 1)

            def body(g, pair):
                for n in range(SLOTS):
                    if has_max(g):
                        maximum(g, pair, 2 * n)
                    for use in chores(g, n):
                        chore(g, pair, use)
                    if n == AT_OUT and has_out(g):
                        region, free = filled(dve, g, pair, ("out", 0))
                        dve.scalar_tensor_tensor(node_t[:, :], flat(region), w_o[:, 2 * D:2 * D + 1], res_sb[:, :],
                                                 ALU.mult, ALU.add).then_inc(free, 1)
                    if n == AT_RDEN and has_out(g):
                        dve.wait_ge(s["den_loaded"], value("out", g, pair, 16, 16))
                        dve.reciprocal(rden[:, :], den[:, :]).then_inc(s["rden_done"], 1)
                    if tail(g):
                        tail_part(g, pair, n)
                    if has_max(g):
                        maximum(g, pair, 2 * n + 1)

            def maximum(g, pair, u):
                region, free = filled(dve, g, pair, ("max", u))
                dve.tensor_reduce(mx[:, u // 32, u % 32 // 4, u % 4:u % 4 + 1], region, AX.XY, ALU.max).then_inc(free, 1)

            iterations(dve, body, G0 + 1)


_INS = ["L0_attn_x", "L0_attn_Wq", "L0_attn_bq", "L0_attn_Wk", "L0_attn_bk", "L0_attn_Wv", "L0_attn_bv", "L0_attn_Wo",
        "L0_attn_bo", "L0_ffn_ew", "L0_ffn_act_w", "L0_ffn_We", "L0_ffn_be", "L0_ffn_Wq", "L0_ffn_Wk", "L0_ffn_Wv",
        "L0_ffn_Wo", "L0_ffn_ln_g", "L0_ffn_ln_b"]


def kernel(**inputs):
    import numpy as np
    import concourse.bacc as bacc
    from concourse.bass_utils import run_bass_kernel_spmd

    nc = bacc.Bacc("TRN2", target_bir_lowering=False, num_devices=1)
    arrays, args = {}, []
    for name in _INS:
        a = np.ascontiguousarray(inputs[name])
        arrays[f"in_{name}"] = a
        args.append(nc.dram_tensor(f"in_{name}", a.shape, mybir.dt.from_np(a.dtype), kind="ExternalInput").ap())
    out = nc.dram_tensor("out", (B, S, D), F32, kind="ExternalOutput").ap()
    preln_attention_cell(nc, *args, out)
    r = run_bass_kernel_spmd(nc, [arrays], core_ids=[0])
    return r.results[0]["out"]
```

```python
from contextlib import ExitStack

from concourse import mybir

F32 = mybir.dt.float32
BF16 = mybir.dt.bfloat16
ALU = mybir.AluOpType
ACT = mybir.ActivationFunctionType
AX = mybir.AxisListType

D = 128
B = 4
S = 1024
NODES = 6
MAX_PREV = 5
HEADS = 8
DH = 16
TERMS = 6
KR = TERMS * DH
KM = KR + 3
GROUP = 4
NB = S // 128
ATTN_STEPS = 2 * B
STEPS = ATTN_STEPS + NODES * B
SLOTS = 32
PRING = 4

AT_MROW1, AT_K, AT_Q1, AT_Q, AT_V, AT_OUT, AT_T1, AT_MROW0, AT_T2 = 1, 2, 4, 6, 11, 15, 17, 20, 29
AT_DEN, AT_RDEN = 2, 8


def has_b(g):
    return 0 <= g < STEPS


def has_max(g):
    return 0 <= g + 1 < STEPS


def has_proj(g):
    return 0 <= g + 2 < STEPS


def has_out(g):
    return 0 <= g - 1 < STEPS


def tail(g):
    s = g - 1
    if 0 <= s < ATTN_STEPS:
        return "mid" if s % 2 else ""
    return "last" if STEPS - B <= s < STEPS else ""


def ring_uses(g):
    uses = []
    for n in range(SLOTS):
        tiles = [[("max", 2 * n)], [("max", 2 * n + 1)]] if has_max(g) else [[], []]
        uses += first_chores(g, n) + tiles[0] + mid_chores(g, n) + tiles[1]
    return uses


def first_chores(g, n):
    return [use for use in chores(g, n) if use[0] == "mrow"]


def mid_chores(g, n):
    return [use for use in chores(g, n) if use[0] != "mrow"]


def chores(g, n):
    out = []
    if n == AT_MROW1 and has_b(g):
        out.append(("mrow", 1))
    if n == AT_K and has_proj(g):
        out.append(("k", 0))
    if n == AT_Q1 and has_proj(g):
        out.append(("q1", 0))
    if n == AT_Q and has_proj(g):
        out.append(("q", 0))
    if n == AT_V and has_max(g):
        out.append(("v", 0))
    if n == AT_OUT and has_out(g):
        out.append(("out", 0))
    if n == AT_T1 and tail(g):
        out.append(("t1", 0))
    if n == AT_MROW0 and has_max(g):
        out.append(("mrow", 0))
    if n == AT_T2 and tail(g) == "mid":
        out.append(("t2", 0))
    return out


def pv_slots(g, n):
    t = n - 2
    return [t] if (has_b(g) if t >= 0 else has_out(g)) else []


G0 = -2


def per_iteration(g):
    b, m, a, o, t = has_b(g), has_max(g), has_proj(g), has_out(g), tail(g)
    return {
        "scores": 4 * SLOTS * b,
        "pv": sum(len(pv_slots(g, n)) for n in range(SLOTS)),
        "acc": 3 * b + o,
        "ring": len(ring_uses(g)),
        "proj": 1 * a,
        "mrow": b + m,
        "out": 1 * o,
        "tail": 1 * bool(t),
        "mid": 1 * (t == "mid"),
        "last": 1 * (t == "last"),
        "loads": 16 * (3 * (has_proj(g) and g > G0) + 2 * has_max(g) + 2 * has_out(g)),
    }


TOTAL = {g: {} for g in range(G0, STEPS + 4)}
for _name in per_iteration(0):
    _n = 0
    for _g in range(G0, STEPS + 4):
        TOTAL[_g][_name] = _n
        _n += per_iteration(_g)[_name]


def value(name, g, pair=None, add=0, times=1):
    v = times * TOTAL[g][name] + add
    if pair is None:
        return v
    return v + times * (TOTAL[g + 2][name] - TOTAL[g][name]) * pair


def wait(eng, sem, v):
    if not isinstance(v, int) or v > 0:
        eng.wait_ge(sem, v)


LOOPS = [(1, 4), (9, 10)]


def iterations(eng, body, first=G0, last=STEPS):
    g = first
    while g <= last:
        loop = next((l for l in LOOPS if l[0] == g), None)
        if loop:
            with eng.Fori(0, loop[1]) as pair:
                body(g, pair)
                body(g + 1, pair)
            g += 2 * loop[1]
        else:
            body(g, None)
            g += 1


def edges():
    first = 0
    out = []
    for c in range(NODES):
        n = min(c + 1, MAX_PREV)
        out.append((first + n - 1, first, first + n // 2))
        first += n
    return out


def preln_attention_cell(nc, x, Wq, bq, Wk, bk, Wv, bv, Wo, bo, ew, act_w, We, be, fWq, fWk, fWv, fWo, ln_g, ln_b, out):
    EDGES = edges()
    N_EDGES = We.shape[0]
    A_COLS = 3 * D + 3
    O_COLS = D + 2
    SETS = 2 + NODES

    def dram(name, shape, dt=F32):
        return nc.dram_tensor(name, shape, dt).ap()

    set_a = dram("set_a", [SETS, D, A_COLS])
    set_v = dram("set_v", [SETS, D, D])
    set_o = dram("set_o", [SETS, D, O_COLS])
    xt = dram("xt", [4 + 4 * NODES, D, S])
    resid = dram("resid", [2 * STEPS, D, S])
    x1_tok = dram("x1_tok", [B, 128, NB, D])
    parts_k = dram("parts_k", [2, 3, HEADS, DH, S], BF16)
    parts_q = dram("parts_q", [2, 3, HEADS, DH, S], BF16)
    dens = dram("dens", [2 * GROUP, S])
    rdens = dram("rdens", [2 * GROUP, S])
    mrows = dram("mrows", [2, 3, GROUP, S], BF16)

    with ExitStack() as ctx:
        def sb(name, shape, dt=F32):
            return ctx.enter_context(nc.sbuf_tensor(name, shape, dt))

        def psum(name, shape):
            return ctx.enter_context(nc.psum_tensor(name, shape, F32))

        def sem(name):
            return ctx.enter_context(nc.semaphore(name))

        k_aug = sb("k_aug", [128, 2, HEADS, S], BF16)
        q_aug = sb("q_aug", [128, 2, HEADS, S], BF16)
        probs = sb("probs", [128, PRING, GROUP, 512])
        v_sb = sb("v_sb", [128, 2, NB, HEADS, 32])
        xk = sb("xk", [128, S])
        xq = sb("xq", [128, S])
        xv = sb("xv", [128, S])
        w_a = sb("w_a", [128, A_COLS])
        w_v = sb("w_v", [128, D])
        w_o = sb("w_o", [128, O_COLS])
        q1 = sb("q1", [128, S])
        k32 = sb("k32", [128, S])
        q32 = sb("q32", [128, S])
        rest = sb("rest", [128, S])
        ksp = sb("ksp", [128, 3, S], BF16)
        qsp = sb("qsp", [128, 3, S], BF16)
        mx = sb("mx", [128, 2, NB, GROUP])
        mrest = sb("mrest", [128, 2, NB, GROUP])
        msp = sb("msp", [128, 2, NB, 3, GROUP], BF16)
        mrow_sb = sb("mrow_sb", [128, 2, S // 4], BF16)
        ctx_t = sb("ctx_t", [128, 2, 2, S])
        den = sb("den", [128, 2 * GROUP * S // 128])
        rden = sb("rden", [128, 2 * GROUP * S // 128])
        rden_b = sb("rden_b", [128, 2, S])
        res_sb = sb("res_sb", [128, S])
        node_t = sb("node_t", [128, S])
        xtok = sb("xtok", [128, NB, D])
        xhat = sb("xhat", [128, NB, D])
        stats = sb("stats", [128, NB, 6])
        mv = sb("mv", [128, NB, 2])
        var = sb("var", [128, NB])
        rest_t = sb("rest_t", [128, S])
        sd = sb("sd", [128, NB])
        rstd = sb("rstd", [128, NB])
        ident = sb("ident", [128, 128])
        identb = sb("identb", [128, 128], BF16)
        gain = sb("gain", [128, D])
        shift = sb("shift", [128, D])

        sc = psum("sc", [128, 3, 512])
        ring = psum("ring", [128, 2, 2, 512])
        acc = psum("acc", [128, 512])

        raw = probs[:, :, :, :].rearrange("p a b c -> p (a b c)")[:, 0:(4 + N_EDGES + 4 * NODES) * D].rearrange(
            "p (m d) -> p m d", d=D)

        def we_raw(c, w):
            return raw[:, 4 + EDGES[c][w], :]

        def w_raw(c, w):
            return raw[:, 4 + N_EDGES + NODES * w + c, :]
        prep = v_sb[:, :, :, :, :].rearrange("p a b c d -> p (a b c d)")
        half_q = q_aug[:, 1, :, :].rearrange("p a b -> p (a b)").bitcast(F32)
        half_k = k_aug[:, 1, :, :].rearrange("p a b -> p (a b)").bitcast(F32)
        st_a = half_q[:, 0:SETS * A_COLS].rearrange("p (s c) -> p s c", s=SETS)
        st_o = half_q[:, SETS * A_COLS:SETS * A_COLS + 2 * O_COLS].rearrange("p (s c) -> p s c", s=2)
        st_v = half_k[:, 0:SETS * D].rearrange("p (s c) -> p s c", s=SETS)
        st_z = half_k[:, SETS * D:SETS * D + NODES * 2].rearrange("p (s c) -> p s c", s=NODES)
        x_in = [ctx_t[:, b // 2, b % 2, :].rearrange("p (k d) -> p k d", k=NB) for b in range(B)]
        x_out = [rden_b[:, 0, :], rden_b[:, 1, :], node_t[:, :], rest_t[:, :]]
        at_we, at_wo, at_woc, at_small, at_brow, at_be = 0, 1536, 1664, 2176, 2304, 3072
        we_t = prep[:, at_we:at_we + 2 * NODES * D].rearrange("p (c w d) -> p c w d", w=2, d=D)
        wo_t = prep[:, at_wo:at_wo + D]
        wo_c = prep[:, at_woc:at_woc + 2 * D].rearrange("p (t a e) -> p t a e", t=2, e=DH)
        small = prep[:, at_small:at_small + 64]
        ew_b, aw_b = small[:, 0:3 * NODES], small[:, 18:18 + NODES]
        bes = small[:, 24:24 + 2 * NODES]
        bvo = small[:, 42:44]
        ones2 = small[:, 44:46]
        ones_col, one = ones2[:, 0:1], ones2[0:1, 0:1]
        brow = prep[0:1, at_brow:at_brow + 4 * D].rearrange("p (w h c) -> p w h c", w=2, h=2)
        be_rows = prep[0:20, at_be:at_be + D]

        names = """prep_in1 prep_in2 prep_x_stored prep_ln prep_jobs prep_evac prep_stored prep_zero prep_cleared
            prep_id prep_x prep_x_rest prep_norm prep_step ones_set consts
            scores_ready exp_done pv_done acc_free ring_full ring_free0 ring_free1
            k_split q_split m_split k_step q_step m_step pool_tick dve_tick sp_tick
            mrow_dram mrow_loaded0 mrow_loaded1 parts_stored aug_loaded0 aug_loaded1
            den_stored den_loaded rden_done rden_stored rden_loaded ctx_done ctx_step q1_stored node_stored loaded x1_loaded
            tok_stored tok_step var_ready sd_done rstd_done xhat_done xt_stored final_step final_stored""".split()
        s = {n: sem(n) for n in names}
        ring_free = [s["ring_free0"], s["ring_free1"]]
        aug_loaded = [s["aug_loaded0"], s["aug_loaded1"]]
        mrow_loaded = [s["mrow_loaded0"], s["mrow_loaded1"]]
        block = ctx.enter_context(nc.Block())

        def ring_use(g, use):
            at = ring_uses(g).index(use)
            return at, (TOTAL[g]["ring"] + at) % 2

        def claim(pe, g, pair, use):
            at, r = ring_use(g, use)
            n = TOTAL[g]["ring"] + at
            v = n // 2
            if pair is not None:
                v = v + (TOTAL[g + 2]["ring"] - TOTAL[g]["ring"]) // 2 * pair
            wait(pe, ring_free[r], v)
            return ring[:, r]

        def filled(eng, g, pair, use):
            at, r = ring_use(g, use)
            eng.wait_ge(s["ring_full"], value("ring", g, pair, at + 1))
            return ring[:, r], ring_free[r]

        def evacuated(eng, g, pair, use):
            at, r = ring_use(g, use)
            v = (TOTAL[g]["ring"] + at) // 2 + 1
            if pair is not None:
                v = v + (TOTAL[g + 2]["ring"] - TOTAL[g]["ring"]) // 2 * pair
            eng.wait_ge(ring_free[r], v)
            if eng.engine == mybir.EngineType.SP and pair is not None:
                eng.sem_inc(s["sp_tick"], 1)

        def evacuated_before(eng, g, pair):
            n = TOTAL[g]["ring"] - 1
            v = n // 2 + 1
            if pair is not None:
                v = v + (TOTAL[g + 2]["ring"] - TOTAL[g]["ring"]) // 2 * pair
            eng.wait_ge(ring_free[n % 2], v)

        def split(eng, tick, src, parts, tmp, step, first, done):
            eng.sem_inc(tick, 1)
            eng.tensor_copy(parts[0], src).then_inc(step, 1)
            eng.wait_ge(step, first + 1)
            eng.tensor_tensor(tmp, src, parts[0], ALU.subtract).then_inc(step, 1)
            eng.wait_ge(step, first + 2)
            eng.sem_inc(tick, 1)
            eng.tensor_copy(parts[1], tmp).then_inc(step, 1)
            eng.wait_ge(step, first + 3)
            eng.tensor_tensor(parts[2], tmp, parts[1], ALU.subtract).then_inc(done, 1)

        def input_loaded(eng, b):
            if b:
                eng.wait_ge(s["prep_x_rest"], 16 * (B - 1))
            else:
                eng.wait_ge(s["prep_x"], 16)

        def flat(region):
            return region.rearrange("p a b -> p (a b)")

        JOBS = [("wt", w) for w in range(3)] + [("bcol", 0), ("x_t", 0), ("xhat_t", 0)]
        FIRST_JOBS = len(JOBS)
        JOBS += [("x_t", 1), ("xhat_t", 1), ("wo_t", 0), ("be", 0)]
        JOBS += [(kind, c) for c in range(NODES) for kind in ("wek_t", "wev_t")] + [("bo", 0)]
        JOBS += [("cols", c) for c in range(NODES)] + [("wo_c", t) for t in range(2)]
        JOBS += [(kind, c) for c in range(NODES) for kind in ("wkk", "wvv")]
        JOBS += [(kind, b) for b in (2, 3) for kind in ("x_t", "xhat_t")]
        job_at = {j: n for n, j in enumerate(JOBS)}

        def job_banks(n):
            return {2 * (n % 2), 2 * (n % 2) + 1} if JOBS[n][0] in ("x_t", "xhat_t") else {n % 4}

        def job_place(n):
            bank = min(job_banks(n))
            return ring[:, bank // 2], ring[:, bank // 2, bank % 2, 0:D]

        def job_after(n):
            kind, i = JOBS[n]
            reads = {"bo": ("wo_t", 0), "wkk": ("wek_t", i), "wvv": ("wev_t", i), "cols": ("be", 0)}
            if kind == "wo_c" and i == 1:
                reads["wo_c"] = ("bo", 0)
            before = [m for m in range(n) if job_banks(m) & job_banks(n)]
            if kind in reads:
                before.append(job_at[reads[kind]])
            return max(before, default=-1) + 1

        N_IN1 = 3 + 4
        N_IN2 = 1 + 7 + 5
        N_STORED1 = 6
        N_STORED = 5

        @block.sync
        def _(sp):
            def load(dst, src, part):
                sp.dma_start(dst, src).then_inc(s[f"prep_in{part}"], 16)

            def x_store(b, what):
                sp.wait_ge(s["prep_evac"], job_at[what, b] + 1)
                dst, m = (resid[2 * b], 2 * b) if what == "x_t" else (xt[b], 2 * b + 1)
                sp.dma_start(dst, x_out[m % 4]).then_inc(s["prep_x_stored"], 16)

            for b in range(B):
                sp.dma_start(x_in[b], x[b].rearrange("(k p) d -> p k d", p=128)).then_inc(s["prep_x_rest" if b else "prep_x"], 16)
                if b == 0:
                    for n, w in enumerate((Wq, Wk, Wv)):
                        load(raw[:, n, :], w, 1)
                    sp.wait_ge(s["prep_zero"], 1)
                    for w, bias in enumerate((bq, bk)):
                        for h in range(2):
                            load(brow[:, w, h, :].rearrange("p (a e) -> p a e", e=DH)[:, :, 0:8],
                                 bias[64 * h:64 * h + 64].rearrange("(o a e) -> o a e", o=1, e=8), 1)
            x_store(0, "x_t")
            x_store(0, "xhat_t")
            for h in range(2):
                sp.dma_start(set_a[h], st_a[:, h, :]).then_inc(s["prep_x_stored"], 16)
                sp.dma_start(set_v[h], st_v[:, h, :]).then_inc(s["prep_x_stored"], 16)
            sp.wait_ge(s["prep_x_stored"], 16 * N_STORED1)

            def second_part():
                x_store(1, "x_t")
                x_store(1, "xhat_t")
                sp.wait_ge(s["prep_step"], 3)
                sp.wait_ge(s["prep_evac"], job_at["wvv", NODES - 1] + 1)
                sp.dma_start(set_a[2:].rearrange("s p c -> p s c"), st_a[:, 2:, :]).then_inc(s["prep_stored"], 16)
                sp.dma_start(set_v[2:].rearrange("s p c -> p s c"), st_v[:, 2:, :]).then_inc(s["prep_stored"], 16)
                sp.dma_start(set_o[0:2].rearrange("s p c -> p s c"), st_o).then_inc(s["prep_stored"], 16)
                sp.dma_start(set_o[2:, :, 0:D].rearrange("c p d -> p c d"),
                             raw[:, 4 + N_EDGES + 3 * NODES:4 + N_EDGES + 4 * NODES, :]).then_inc(s["prep_stored"], 16)
                sp.dma_start(set_o[2:, :, D:].rearrange("c p w -> p c w"), st_z).then_inc(s["prep_stored"], 16)
                sp.wait_ge(s["prep_x_stored"], 16 * (N_STORED1 + 2))
                for b in (2, 3):
                    x_store(b, "x_t")
                    x_store(b, "xhat_t")
                sp.wait_ge(s["prep_stored"], 16 * N_STORED)
                sp.wait_ge(s["prep_x_stored"], 16 * (N_STORED1 + 6))

            def hold(eng, sem_, v):
                wait(eng, sem_, v)
                if not isinstance(v, int):
                    eng.sem_inc(s["sp_tick"], 1)

            def weight_set(step):
                if isinstance(step, int):
                    return step % 2 if step < ATTN_STEPS else 2 + (step - ATTN_STEPS) // B
                return (step - ATTN_STEPS) // B + 2

            def source(step, which):
                if isinstance(step, int) and step < ATTN_STEPS:
                    return step // 2
                t = step - ATTN_STEPS
                c, b = t // B, t % B
                if which == "q":
                    return t + 4
                if which == "k":
                    return (c + 3) // 8 * 4 + b + 4
                return (c + 1) // 2 * 4 + b + 4

            def loads_for(g, pair):
                if has_proj(g):
                    st = g + 2 if pair is None else pair * 2 + (g + 2)
                    sp.dma_start(xk[:, :], xt[source(st, "k")]).then_inc(s["loaded"], 16)
                    sp.dma_start(xq[:, :], xt[source(st, "q")]).then_inc(s["loaded"], 16)
                    sp.dma_start(w_a[:, :], set_a[weight_set(st)]).then_inc(s["loaded"], 16)
                if has_max(g):
                    st = g + 1 if pair is None else pair * 2 + (g + 1)
                    sp.dma_start(xv[:, :], xt[source(st, "v")]).then_inc(s["loaded"], 16)
                    sp.dma_start(w_v[:, :], set_v[weight_set(st)]).then_inc(s["loaded"], 16)
                if has_out(g):
                    st = g - 1 if pair is None else pair * 2 + (g - 1)
                    sp.dma_start(w_o[:, :], set_o[weight_set(st)]).then_inc(s["loaded"], 16)
                    at = st if g - 1 < ATTN_STEPS else st + STEPS
                    sp.dma_start(res_sb[:, :], resid[at]).then_inc(s["loaded"], 16)

            def aug_loads(g, hg):
                par = g % 2
                heads = slice(GROUP * hg, GROUP * hg + GROUP)
                src_k = parts_k[par].rearrange("a (j g) d t -> g a d j t", g=2)[hg]
                src_q = parts_q[par].rearrange("a (j g) d t -> g a d j t", g=2)[hg]
                for t, (pk, pq) in enumerate([(0, 0), (0, 1), (0, 2), (1, 0), (1, 1), (2, 0)]):
                    sp.dma_start(k_aug[DH * t:DH * t + DH, par, heads, :], src_k[pk]).then_inc(aug_loaded[hg], 16)
                    sp.dma_start(q_aug[DH * t:DH * t + DH, par, heads, :], src_q[pq]).then_inc(aug_loaded[hg], 16)

            def mrow_move(g, pair, hg, par, done, before):
                evacuated(sp, g, pair, ("mrow", hg))
                hold(sp, mrow_loaded[hg], before)
                for c in range(4):
                    sp.dma_start(mrows[hg].rearrange("a h t -> (a h) t")[:, 256 * c:256 * c + 256],
                                 mrow_sb[32 * c:32 * c + 3 * GROUP, hg, :]).then_inc(s["mrow_dram"], 16)
                hold(sp, s["mrow_dram"], done * 64)
                sp.dma_start(q_aug[KR:KM, par, GROUP * hg:GROUP * hg + GROUP, :], mrows[hg]).then_inc(mrow_loaded[hg], 16)

            def mrow_loads(g, pair, hg):
                v = 16 * (g if hg else g + 1)
                return v if pair is None else pair * 32 + v

            def body(g, pair):
                par = g % 2
                if tail(g) == "last":
                    hold(sp, s["final_step"], value("last", g, pair, 0, 3))
                    sp.dma_start(res_tok, x1_tok[(g - 1) % B]).then_inc(s["x1_loaded"], 16)
                if has_out(g):
                    hold(sp, s["acc_free"], value("acc", g, pair, 1))
                    for hg in range(2):
                        sp.dma_start(dens[GROUP * hg:GROUP * hg + GROUP, :],
                                     ctx_t[DH * (1 - hg):128:32, 1 - par, hg, :]).then_inc(s["den_stored"], 16)
                    hold(sp, s["den_stored"], value("out", g, pair, 32, 32))
                    sp.dma_start(den[:, :], dens.rearrange("h (a t) -> (h a) t", a=16)).then_inc(s["den_loaded"], 16)
                if has_b(g):
                    mrow_move(g, pair, 1, par, value("mrow", g, pair, 1), mrow_loads(g, pair, 1))
                if has_out(g):
                    hold(sp, s["rden_done"], value("out", g, pair, 1))
                    sp.dma_start(rdens.rearrange("h (a t) -> (h a) t", a=16), rden[:, :]).then_inc(s["rden_stored"], 16)
                    hold(sp, s["rden_stored"], value("out", g, pair, 16, 16))
                    if g == 1:
                        sp.wait_ge(s["consts"], 3)
                    for h in range(HEADS):
                        src = rdens[GROUP * (h % 2) + h // 2:GROUP * (h % 2) + h // 2 + 1]
                        sp.dma_start(rden_b[DH * h:DH * h + DH, h % 2, :], src.broadcast_to([DH, S])).then_inc(s["rden_loaded"], 16)
                if has_proj(g):
                    st = g + 2 if pair is None else pair * 2 + (g + 2)
                    evacuated(sp, g, pair, ("q1", 0))
                    sp.dma_start(resid[st + STEPS], q1[:, :]).then_inc(s["q1_stored"], 16)
                    hold(sp, s["k_split"], value("proj", g, pair, 1))
                    sp.dma_start(parts_k[par].rearrange("a h d t -> (h d) a t"), ksp[:, :, :]).then_inc(s["parts_stored"], 16)
                    hold(sp, s["q_split"], value("proj", g, pair, 1))
                    sp.dma_start(parts_q[par].rearrange("a h d t -> (h d) a t"), qsp[:, :, :]).then_inc(s["parts_stored"], 16)
                if has_out(g):
                    evacuated(sp, g, pair, ("out", 0))
                    st = g - 1 if pair is None else pair * 2 + (g - 1)
                    if tail(g) == "":
                        if g - 1 < ATTN_STEPS:
                            sp.dma_start(resid[st + 1], node_t[:, :]).then_inc(s["node_stored"], 16)
                        else:
                            sp.dma_start(xt[st], node_t[:, :]).then_inc(s["node_stored"], 16)
                if has_proj(g):
                    hold(sp, s["parts_stored"], value("proj", g, pair, 32, 32))
                    if has_b(g):
                        hold(sp, s["scores_ready"], value("scores", g, pair, 64))
                    aug_loads(g, 0)
                if has_max(g):
                    mrow_move(g, pair, 0, 1 - par, value("mrow", g, pair, 1 + has_b(g)), mrow_loads(g, pair, 0))
                if tail(g):
                    b = (g - 1) // 2 if pair is None else pair + (g - 1) // 2
                    if tail(g) == "mid":
                        evacuated(sp, g, pair, ("t1", 0))
                        sp.dma_start(x1_tok[b], xtok[:, :, :]).then_inc(s["tok_stored"], 16)
                        evacuated(sp, g, pair, ("t2", 0))
                        sp.dma_start(xt[b + 4], rest2).then_inc(s["xt_stored"], 16)
                    else:
                        hold(sp, s["final_step"], value("last", g, pair, 3, 3))
                        sp.dma_start(out[(g - 1) % B].rearrange("(k p) d -> p k d", p=128), xhat[:, :, :]).then_inc(s["final_stored"], 16)
                if g == G0:
                    aug_loads(g, 1)
                if g < STEPS:
                    n = g + 1
                    if has_proj(g):
                        evacuated(sp, g, pair, ("q", 0))
                        hold(sp, s["q1_stored"], value("proj", g, pair, 16, 16))
                    if has_max(g):
                        evacuated(sp, g, pair, ("v", 0))
                    if has_out(g):
                        evacuated(sp, g, pair, ("out", 0))
                    if has_out(g) and tail(g) == "":
                        hold(sp, s["node_stored"], node_value(g, pair))
                    if tail(g) == "mid":
                        hold(sp, s["xt_stored"], value("mid", g, pair, 16, 16))
                        hold(sp, s["tok_stored"], value("mid", g, pair, 16, 16))
                    loads_for(n, pair)
                    if g == G0:
                        second_part()
                if has_proj(g) and g > G0:
                    if has_b(g):
                        hold(sp, s["scores_ready"], value("scores", g, pair, 128))
                    aug_loads(g, 1)

            def node_value(g, pair):
                n = sum(1 for i in range(G0, g + 1) if has_out(i) and tail(i) == "")
                if pair is None:
                    return 16 * n
                per = sum(1 for i in (g + 1, g + 2) if has_out(i) and tail(i) == "")
                return 16 * n + 16 * per * pair

            rest2 = rest_t[:, :]
            res_tok = rest_t[:, :].rearrange("p (k d) -> p k d", k=NB)
            load(raw[:, 3, :], Wo, 2)
            load(be_rows, be, 2)
            load(bvo[:, 0:1], bv.rearrange("(d o) -> d o", o=1), 2)
            load(bvo[:, 1:2], bo.rearrange("(d o) -> d o", o=1), 2)
            load(ew_b, ew.rearrange("(o c) w -> o (c w)", o=1).partition_broadcast(128), 2)
            load(aw_b, act_w.rearrange("(o c) -> o c", o=1).partition_broadcast(128), 2)
            load(gain[:, :], ln_g.rearrange("(o c) -> o c", o=1).partition_broadcast(128), 2)
            load(shift[:, :], ln_b.rearrange("(o c) -> o c", o=1).partition_broadcast(128), 2)
            load(raw[:, 4:4 + N_EDGES, :], We.rearrange("e p d -> p e d"), 2)
            for n, w in enumerate((fWq, fWk, fWv, fWo)):
                at = 4 + N_EDGES + NODES * n
                load(raw[:, at:at + NODES, :], w.rearrange("c p d -> p c d"), 2)
            for g in range(G0, LOOPS[1][0]):
                body(g, None)
            iterations(sp, body, LOOPS[1][0])
            hold(sp, s["final_stored"], 16 * B)
            hold(sp, s["node_stored"], node_value(STEPS, None))
            hold(sp, s["mrow_dram"], value("mrow", STEPS, None, 0, 64))

        @block.tensor
        def _(pe):
            def jobs(first, last_job):
                for n in range(first, last_job):
                    kind, i = JOBS[n]
                    region, out1 = job_place(n)
                    wait(pe, s["prep_evac"], job_after(n))
                    if kind == "be":
                        last = pe.transpose(out1[:, 0:20], be_rows, ident[0:20, 0:20])
                    elif kind == "wt":
                        last = pe.transpose(out1, raw[:, i, :], ident[:, :])
                    elif kind == "bcol":
                        for w in range(2):
                            for h in range(2):
                                last = pe.matmul(out1[:, 2 * w + h:2 * w + h + 1], brow[:, w, h, :], one, start=True, stop=True)
                    elif kind == "wo_t":
                        last = pe.transpose(out1, raw[:, 3, :], ident[:, :])
                    elif kind == "bo":
                        last = pe.matmul(out1[:, 0:1], wo_t, bvo[:, 0:1], start=True, stop=True)
                    elif kind == "wo_c":
                        pe.wait_ge(s["prep_step"], 2)
                        last = pe.transpose(out1, wo_c[:, i].rearrange("p a e -> p (a e)"), ident[:, :])
                    elif kind in ("wek_t", "wev_t"):
                        last = pe.transpose(out1, we_raw(i, 1 if kind == "wek_t" else 2), ident[:, :])
                    elif kind in ("wkk", "wvv"):
                        w = 0 if kind == "wkk" else 1
                        last = pe.matmul(out1, we_t[:, i, w], w_raw(i, 1 + w), start=True, stop=True)
                    elif kind == "cols":
                        pe.matmul(out1[:, 0:1], w_raw(i, 1), bes[:, 2 * i:2 * i + 1], start=True, stop=True)
                        last = pe.matmul(out1[:, 1:2], w_raw(i, 2), bes[:, 2 * i + 1:2 * i + 2], start=True, stop=True)
                    else:
                        if kind == "x_t":
                            input_loaded(pe, i)
                        else:
                            pe.wait_ge(s["prep_norm"], i + 1)
                        src = x_in[i] if kind == "x_t" else xhat
                        for k in range(NB):
                            last = pe.transpose(region[:, k // 4, 128 * (k % 4):128 * (k % 4) + 128], src[:, k, :], ident[:, :])
                    last.then_inc(s["prep_jobs"], 1)

            def project(g, pair, use, w, src):
                region = claim(pe, g, pair, use)
                for half in range(2):
                    last = pe.matmul(region[:, half, :], w, src[:, 512 * half:512 * half + 512], start=True, stop=True)
                last.then_inc(s["ring_full"], 1)

            def chore(g, pair, use):
                kind, hg = use
                w, src_k, src_q = (w_a, xk, xq) if g > G0 else (st_a[:, 0, :], x_out[1], x_out[1])
                if kind == "k":
                    wait(pe, s["loaded"], value("loads", g + 1, pair))
                    project(g, pair, use, w[:, 2 * D:3 * D], src_k)
                elif kind == "q1":
                    project(g, pair, use, w[:, 0:D], src_q)
                elif kind == "q":
                    evacuated(pe, g, pair, ("q1", 0))
                    project(g, pair, use, w[:, D:2 * D], q1)
                elif kind == "v":
                    pe.wait_ge(s["loaded"], value("loads", g + 1, pair))
                    region = claim(pe, g, pair, use)
                    for k in range(NB):
                        last = pe.matmul(region[:, k // 4, 128 * (k % 4):128 * (k % 4) + 128],
                                         xv[:, 128 * k:128 * k + 128], w_v[:, :], start=True, stop=True)
                    last.then_inc(s["ring_full"], 1)
                elif kind == "mrow":
                    done = value("mrow", g, pair, 1 if hg else 1 + has_b(g))
                    pe.wait_ge(s["m_split"], done)
                    region = claim(pe, g, pair, use)
                    for k in range(NB):
                        last = pe.matmul(region[32 * (k // 2):32 * (k // 2) + 3 * GROUP, 0, 128 * (k % 2):128 * (k % 2) + 128],
                                         msp[:, hg, k].rearrange("p a h -> p (a h)"), identb[:, :], start=True, stop=True)
                    last.then_inc(s["ring_full"], 1)
                elif kind == "out":
                    pe.wait_ge(s["loaded"], value("loads", g + 1, pair))
                    pe.wait_ge(s["ctx_done"], value("out", g, pair, 1))
                    region = claim(pe, g, pair, use)
                    for half in range(2):
                        last = pe.matmul(region[:, half, :], w_o[:, 0:D], ctx_t[:, (g - 1) % 2, 0, 512 * half:512 * half + 512], start=True, stop=True)
                    last.then_inc(s["ring_full"], 1)
                else:
                    if kind == "t1":
                        evacuated(pe, g, pair, ("out", 0))
                    else:
                        pe.wait_ge(s["xhat_done"], value("tail", g, pair, 1))
                    region = claim(pe, g, pair, use)
                    for k in range(NB):
                        src = node_t[:, 128 * k:128 * k + 128] if kind == "t1" else xhat[:, k, :]
                        last = pe.transpose(region[:, k // 4, 128 * (k % 4):128 * (k % 4) + 128], src, ident[:, :])
                    last.then_inc(s["ring_full"], 1)

            def score(g, pair, n, j):
                i = 4 * n + j
                before = i - 2 if i >= 3 else (-1, 0, -2)[i]
                wait(pe, s["exp_done"], value("scores", g, pair, before))
                hg, qh, kc = n // 16, n // 8 % 2, n % 8
                h = GROUP * hg + j
                pe.matmul(sc[:, i % 3, :], k_aug[0:KM, g % 2, h, 128 * kc:128 * kc + 128],
                          q_aug[0:KM, g % 2, h, 512 * qh:512 * qh + 512], start=True, stop=True).then_inc(s["scores_ready"], 1)

            def max_scores(g, pair, u):
                hg, qb, h = u // 32, u % 32 // 4, u // 32 * GROUP + u % 4
                region = claim(pe, g, pair, ("max", u))
                par = (g + 1) % 2
                for half in range(2):
                    last = pe.matmul(region[:, half, :], q_aug[0:KR, par, h, 128 * qb:128 * qb + 128],
                                     k_aug[0:KR, par, h, 512 * half:512 * half + 512], start=True, stop=True)
                last.then_inc(s["ring_full"], 1)

            def pv(g, pair, t):
                par, t_in = (g % 2, t) if t >= 0 else ((g - 1) % 2, t + SLOTS)
                hg, kc = t_in // 16, t_in % 8
                pe.wait_ge(s["exp_done"], value("scores", g, pair, 4 * (t + 1)))
                if kc == 0:
                    wait(pe, s["acc_free"], value("acc", g, pair, t_in // 8 + has_out(g)))
                for j in range(GROUP):
                    last = pe.matmul(acc[32 * j:32 * j + 32, :], v_sb[:, par, kc, GROUP * hg + j, :],
                                     probs[:, t_in % PRING, j, :], start=kc == 0, stop=kc == 7)
                last.then_inc(s["pv_done"], 1)

            def body(g, pair):
                for n in range(SLOTS):
                    if has_max(g) and n % 16 == 0:
                        pe.wait_ge(aug_loaded[n // 16], aug_value(g, pair))
                    if has_b(g) and n % 16 == 0:
                        pe.wait_ge(mrow_loaded[n // 16], mrow_value(g, pair))
                    for half in range(2):
                        for use in (first_chores, mid_chores)[half](g, n):
                            chore(g, pair, use)
                        if has_b(g):
                            score(g, pair, n, 2 * half)
                            score(g, pair, n, 2 * half + 1)
                        if has_max(g):
                            max_scores(g, pair, 2 * n + half)
                    for t in pv_slots(g, n):
                        pv(g, pair, t)

            def aug_value(g, pair):
                v = 16 * 2 * TERMS * (g + 2)
                return v if pair is None else v + 16 * 2 * TERMS * 2 * pair

            def mrow_value(g, pair):
                return 16 * (g + 1) if pair is None else pair * 32 + 16 * (g + 1)

            pe.wait_ge(s["prep_id"], 3)
            pe.wait_ge(s["prep_in1"], 16 * N_IN1)
            pe.wait_ge(s["prep_step"], 1)
            jobs(0, FIRST_JOBS)
            pe.wait_ge(s["prep_evac"], FIRST_JOBS)
            body(G0, None)
            evacuated(pe, G0, None, ("q1", 0))
            evacuated(pe, G0, None, ("q", 0))
            jobs(FIRST_JOBS, job_at["wo_t", 0])
            pe.wait_ge(s["prep_in2"], 16 * N_IN2)
            jobs(job_at["wo_t", 0], len(JOBS))
            pe.wait_ge(s["prep_evac"], len(JOBS))
            body(G0 + 1, None)
            pe.wait_ge(s["consts"], 2)
            pe.wait_ge(s["ones_set"], 4)
            iterations(pe, body, G0 + 2)

        @block.scalar
        def _(act):
            def deviation(b):
                act.wait_ge(s["var_ready"], b + 1)
                act.activation(sd[:, :], var[:, :], ACT.Sqrt).then_inc(s["sd_done"], 1)

            def chore(g, pair, use):
                if use[0] == "t2":
                    region, free = filled(act, g, pair, use)
                    act.activation(rest_t[:, :], flat(region), ACT.Copy).then_inc(free, 1)
                elif use[0] == "mrow":
                    region, free = filled(act, g, pair, use)
                    act.activation(mrow_sb[0:96 + 3 * GROUP, use[1], :], region[0:96 + 3 * GROUP, 0, 0:S // 4],
                                   ACT.Copy).then_inc(free, 1)

            def body(g, pair):
                for n in range(SLOTS):
                    for use in first_chores(g, n):
                        chore(g, pair, use)
                    if has_b(g):
                        if n >= PRING or has_out(g):
                            act.wait_ge(s["pv_done"], value("pv", g, pair, n - PRING + 1 + 2 * has_out(g)))
                        for j in range(GROUP):
                            if j == 1:
                                contexts(g, pair, n)
                            i = 4 * n + j
                            act.wait_ge(s["scores_ready"], value("scores", g, pair, i + 1))
                            act.activation(probs[:, n % PRING, j, :], sc[:, i % 3, :], ACT.Exp).then_inc(s["exp_done"], 1)
                    else:
                        contexts(g, pair, n)
                    for use in mid_chores(g, n):
                        chore(g, pair, use)
                    if tail(g) and n == AT_T1 + 6:
                        act.wait_ge(s["var_ready"], value("tail", g, pair, B + 1))
                        act.activation(sd[:, :], var[:, :], ACT.Sqrt).then_inc(s["sd_done"], 1)

            def contexts(g, pair, n):
                if n == AT_DEN and has_out(g):
                    context(g, pair, (g - 1) % 2, 3, 2)
                if n in (10, 18, 26) and has_b(g):
                    q = n // 8 - 1
                    context(g, pair, g % 2, q, 8 * (q + 1) + 2 * has_out(g))

            def context(g, pair, par, q, pvs):
                act.wait_ge(s["pv_done"], value("pv", g, pair, pvs))
                act.activation(ctx_t[:, par, q // 2, 512 * (q % 2):512 * (q % 2) + 512], acc[:, :],
                               ACT.Copy).then_inc(s["acc_free"], 1)

            deviation(0)
            body(G0, None)
            for b in range(1, B):
                deviation(b)
            act.wait_ge(s["prep_evac"], len(JOBS))
            act.wait_ge(s["prep_stored"], 16 * N_STORED)
            act.wait_ge(s["prep_x_stored"], 16 * (N_STORED1 + 6))
            iterations(act, body, G0 + 1)

        @block.gpsimd
        def _(pool):
            pool.memset(ident[:, :], 0.0).then_inc(s["prep_id"], 1)
            pool.wait_ge(s["prep_id"], 1)
            pool.affine_select(out=ident[:, :], in_=ident[:, :], compare_op=ALU.not_equal, fill=1.0, base=0,
                               pattern=[[-1, 128]], channel_multiplier=1).then_inc(s["prep_id"], 1)
            pool.wait_ge(s["prep_id"], 2)
            pool.tensor_copy(identb[:, :], ident[:, :]).then_inc(s["prep_id"], 1)
            pool.wait_ge(s["prep_id"], 3)
            pool.memset(k_aug[KR:KM, 0, :, :], -1.0).then_inc(s["consts"], 1)
            pool.wait_ge(s["consts"], 1)

            def m_split(g, pair, hg, nth):
                if hg:
                    evacuated_before(pool, g, pair)
                else:
                    evacuated(pool, g, pair, ("max", 31))
                split(pool, s["pool_tick"], mx[:, hg], [msp[:, hg, :, a, :] for a in range(3)], mrest[:, hg], s["m_step"],
                      value("mrow", g, pair, 3 * nth, 3), s["m_split"])

            def context(g, pair):
                wait(pool, s["k_split"], value("proj", g, pair, int(has_proj(g))))
                pool.wait_ge(s["rden_loaded"], value("out", g, pair, 16 * HEADS, 16 * HEADS))
                part = ctx_t[:, (g - 1) % 2, :, :]
                pool.tensor_tensor(part, part, rden_b[:, :, :], ALU.mult).then_inc(s["ctx_step"], 1)
                pool.wait_ge(s["ctx_step"], value("out", g, pair, 1, 2))
                pool.tensor_tensor(part[:, 0, :], part[:, 0, :], part[:, 1, :], ALU.add).then_inc(s["ctx_step"], 1)
                pool.wait_ge(s["ctx_step"], value("out", g, pair, 2, 2))
                pool.wait_ge(s["loaded"], value("loads", g + 1, pair))
                pool.tensor_tensor(part[:, 0, :], part[:, 0, :], w_o[:, D + 1:D + 2].broadcast_to([128, S]),
                                   ALU.add).then_inc(s["ctx_done"], 1)

            def body(g, pair):
                if has_b(g):
                    m_split(g, pair, 1, 0)
                if has_proj(g):
                    for use, src, parts, step, done in (("k", k32, ksp, "k_step", "k_split"), ("q", q32, qsp, "q_step", "q_split")):
                        if use == "k" and g == G0:
                            continue
                        evacuated(pool, g, pair, (use, 0))
                        if g > G0:
                            pool.wait_ge(s["parts_stored"], value("proj", g, pair, 0, 32))
                        if use == "q" and g > G0:
                            pool.wait_ge(s["k_split"], value("proj", g, pair, 1))
                            if has_out(g):
                                pool.wait_ge(s["ctx_done"], value("out", g, pair, 1))
                        split(pool, s["pool_tick"], src[:, :], [parts[:, a, :] for a in range(3)], rest[:, :], s[step],
                              value("proj", g, pair, 0, 3), s[done])
                        if use == "k" and has_out(g):
                            context(g, pair)
                elif has_out(g):
                    context(g, pair)
                if has_max(g):
                    m_split(g, pair, 0, int(has_b(g)))

            body(G0, None)
            pool.wait_ge(s["q_split"], 1)
            pool.wait_ge(s["prep_evac"], len(JOBS))
            pool.wait_ge(s["prep_stored"], 16 * N_STORED)
            for n in range(4):
                wait(pool, s["ones_set"], n)
                hg = n % 2
                pool.memset(v_sb[:, n // 2, :, GROUP * hg:GROUP * hg + GROUP, DH * (1 - hg):DH * (2 - hg)], 1.0).then_inc(s["ones_set"], 1)
            pool.wait_ge(s["ones_set"], 4)
            pool.memset(k_aug[KR:KM, 1, :, :], -1.0).then_inc(s["consts"], 1)
            pool.wait_ge(s["consts"], 2)
            pool.wait_ge(s["prep_x_stored"], 16 * (N_STORED1 + 6))
            pool.memset(rden_b[:, :, :], 0.0).then_inc(s["consts"], 1)
            pool.wait_ge(s["consts"], 3)
            iterations(pool, body, G0 + 1)

        @block.vector
        def _(dve):
            dve.memset(prep[:, :], 0.0).then_inc(s["prep_zero"], 1)
            dve.memset(st_a[:, :, :], 0.0).then_inc(s["prep_cleared"], 1)
            dve.memset(half_k[:, 0:SETS * D], 0.0).then_inc(s["prep_cleared"], 1)
            dve.wait_ge(s["prep_zero"], 1)
            dve.wait_ge(s["prep_cleared"], 2)
            dve.memset(ones2, 1.0).then_inc(s["prep_step"], 1)
            dve.wait_ge(s["prep_id"], 2)
            for h in range(2):
                dve.tensor_copy(st_a[:, h, 0:D], ident[:, :])

            def chore(g, pair, use):
                kind, hg = use
                if kind not in ("k", "q1", "q", "v"):
                    return
                region, free = filled(dve, g, pair, use)
                if kind == "v":
                    if g == G0 + 1:
                        dve.wait_ge(s["prep_stored"], 16 * N_STORED)
                    for hg in range(2):
                        last = dve.tensor_copy(v_sb[:, (g + 1) % 2, :, GROUP * hg:GROUP * hg + GROUP, DH * hg:DH * hg + DH],
                                               flat(region).rearrange("p (k j g e) -> p k j g e", k=NB, g=2, e=DH)[:, :, :, hg, :])
                    last.then_inc(free, 1)
                else:
                    tile, col = {"q1": (q1, 0), "q": (q32, 1), "k": (k32, 2)}[kind]
                    w = w_a if g > G0 else st_a[:, 0, :]
                    dve.tensor_scalar(tile[:, :], flat(region), w[:, 3 * D + col:3 * D + col + 1], None,
                                      ALU.add).then_inc(free, 1)

            def second_operands():
                dve.wait_ge(s["prep_in2"], 16 * N_IN2)
                dve.wait_ge(s["prep_step"], 1)
                for h in range(2):
                    dve.tensor_copy(st_o[:, h, D:D + 1], ones_col)
                    dve.tensor_copy(st_o[:, h, D + 1:], ident[:, 8:9])
                    last = dve.tensor_copy(wo_c[:, h, :, 0:8], raw[:, 3, 64 * h:64 * h + 64].rearrange("p (a e) -> p a e", e=8))
                last.then_inc(s["prep_step"], 1)
                for c in range(NODES):
                    dve.tensor_scalar(st_a[:, 2 + c, 0:D], we_raw(c, 0), ew_b[:, 3 * c:3 * c + 1], None, ALU.mult)
                    dve.tensor_scalar(st_a[:, 2 + c, D:2 * D], w_raw(c, 0), DH ** -0.5, None, ALU.mult)
                    last = dve.tensor_copy(st_z[:, c, 0:1], aw_b[:, c:c + 1])
                last.then_inc(s["prep_step"], 1)

            factor = 8 ** -0.5
            for n, (kind, i) in enumerate(JOBS):
                region, out1 = job_place(n)
                if n == FIRST_JOBS:
                    for use in ring_uses(G0):
                        chore(G0, None, use)
                    evacuated(dve, G0, None, ("k", 0))
                    split(dve, s["dve_tick"], k32[:, :], [ksp[:, a, :] for a in range(3)], res_sb[:, :], s["k_step"], 0, s["k_split"])
                if n == job_at["wo_t", 0]:
                    second_operands()
                if kind == "x_t":
                    input_loaded(dve, i)
                    for k in range(NB):
                        last = dve.bn_stats(stats[:, k, :], x_in[i][:, k, :])
                    last.then_inc(s["prep_ln"], 1)
                    dve.wait_ge(s["prep_ln"], 1 + 3 * i)
                    for k in range(NB):
                        last = dve.bn_aggr(mv[:, k, :], stats[:, k, :])
                    last.then_inc(s["prep_ln"], 1)
                    dve.wait_ge(s["prep_ln"], 2 + 3 * i)
                    dve.tensor_scalar(var[:, :], mv[:, :, 1], 1e-5, None, ALU.add).then_inc(s["var_ready"], 1)
                    dve.wait_ge(s["sd_done"], i + 1)
                    dve.reciprocal(rstd[:, :], sd[:, :]).then_inc(s["prep_ln"], 1)
                    dve.wait_ge(s["prep_ln"], 3 + 3 * i)
                    for k in range(NB):
                        last = dve.tensor_scalar(xhat[:, k, :], x_in[i][:, k, :], mv[:, k, 0:1], rstd[:, k:k + 1], ALU.subtract, ALU.mult)
                    last.then_inc(s["prep_norm"], 1)
                dve.wait_ge(s["prep_jobs"], n + 1)
                if kind == "be":
                    for c, edge in enumerate(EDGES):
                        for w, dst in ((1, bes[:, 2 * c:2 * c + 1]), (2, bes[:, 2 * c + 1:2 * c + 2]),
                                       (0, st_a[:, 2 + c, 3 * D:3 * D + 1])):
                            e = edge[w]
                            last = dve.tensor_scalar(dst, out1[:, e:e + 1], ew_b[:, 3 * c + w:3 * c + w + 1], None, ALU.mult)
                elif kind == "wt":
                    for h in range(2):
                        src = out1[:, 64 * h:64 * h + 64].rearrange("p (a e) -> p a e", e=8)
                        if i == 2:
                            dst = st_v[:, h, :]
                        else:
                            dst = st_a[:, h, D * (1 + i):D * (2 + i)]
                        last = dve.tensor_scalar(dst.rearrange("p (a e) -> p a e", e=DH)[:, :, 0:8], src,
                                                 factor if i == 0 else 1.0, None, ALU.mult)
                elif kind == "bcol":
                    for w in range(2):
                        for h in range(2):
                            last = dve.tensor_scalar(st_a[:, h, 3 * D + 1 + w:3 * D + 2 + w], out1[:, 2 * w + h:2 * w + h + 1],
                                                     1.0 if w else factor, None, ALU.mult)
                elif kind == "wo_t":
                    last = dve.tensor_copy(wo_t, out1)
                elif kind == "bo":
                    dve.wait_ge(s["prep_step"], 2)
                    last = dve.tensor_tensor(wo_c[:, 1, 0, 8:9], out1[:, 0:1], bvo[:, 1:2], ALU.add)
                elif kind == "wo_c":
                    last = dve.tensor_copy(st_o[:, i, 0:D], out1)
                elif kind == "wek_t":
                    last = dve.tensor_scalar(we_t[:, i, 0], out1, ew_b[:, 3 * i + 1:3 * i + 2], None, ALU.mult)
                elif kind == "wev_t":
                    last = dve.tensor_scalar(we_t[:, i, 1], out1, ew_b[:, 3 * i + 2:3 * i + 3], None, ALU.mult)
                elif kind == "wkk":
                    last = dve.tensor_copy(st_a[:, 2 + i, 2 * D:3 * D], out1)
                elif kind == "wvv":
                    last = dve.tensor_copy(st_v[:, 2 + i, :], out1)
                elif kind == "cols":
                    dve.tensor_copy(st_a[:, 2 + i, 3 * D + 2:3 * D + 3], out1[:, 0:1])
                    last = dve.tensor_copy(st_z[:, i, 1:2], out1[:, 1:2])
                elif kind == "x_t":
                    if i >= 2:
                        dve.wait_ge(s["prep_x_stored"], 16 * (N_STORED1 + 2 * (i - 2)))
                    last = dve.tensor_copy(x_out[2 * i % 4], flat(region))
                else:
                    last = dve.tensor_copy(x_out[(2 * i + 1) % 4], flat(region))
                last.then_inc(s["prep_evac"], 1)

            def tail_part(g, pair, n):
                k0 = n - AT_T1
                if k0 == 0:
                    region, free = filled(dve, g, pair, ("t1", 0))
                    dve.tensor_copy(xtok[:, :, :].rearrange("p k d -> p (k d)"), flat(region)).then_inc(free, 1)
                elif 1 <= k0 <= 4:
                    if k0 == 1:
                        evacuated(dve, g, pair, ("t1", 0))
                    for k in (2 * k0 - 2, 2 * k0 - 1):
                        last = dve.bn_stats(stats[:, k, :], xtok[:, k, :])
                    if k0 == 4:
                        last.then_inc(s["tok_step"], 1)
                elif k0 == 5:
                    dve.wait_ge(s["tok_step"], value("tail", g, pair, 1, 2))
                    dve.sem_inc(s["dve_tick"], 1)
                    for k in range(NB):
                        last = dve.bn_aggr(mv[:, k, :], stats[:, k, :])
                    last.then_inc(s["tok_step"], 1)
                    dve.wait_ge(s["tok_step"], value("tail", g, pair, 2, 2))
                    dve.tensor_scalar(var[:, :], mv[:, :, 1], 1e-5 if tail(g) == "mid" else 1e-6, None,
                                      ALU.add).then_inc(s["var_ready"], 1)
                elif k0 == 8:
                    dve.wait_ge(s["sd_done"], value("tail", g, pair, B + 1))
                    dve.reciprocal(rstd[:, :], sd[:, :]).then_inc(s["rstd_done"], 1)
                    dve.wait_ge(s["rstd_done"], value("tail", g, pair, 1))
                    if tail(g) == "last":
                        wait(dve, s["final_stored"], value("last", g, pair, 0, 16))
                    for k in range(NB):
                        last = dve.tensor_scalar(xhat[:, k, :], xtok[:, k, :], mv[:, k, 0:1], rstd[:, k:k + 1], ALU.subtract, ALU.mult)
                    last.then_inc(s["xhat_done"], 1)
                elif k0 == 10 and tail(g) == "last":
                    dve.wait_ge(s["xhat_done"], value("tail", g, pair, 1))
                    dve.tensor_tensor(xhat[:, :, :], xhat[:, :, :], gain[:, :].rearrange("p (o d) -> p o d", o=1).broadcast_to([128, NB, D]),
                                      ALU.mult).then_inc(s["final_step"], 1)
                    dve.wait_ge(s["final_step"], value("last", g, pair, 1, 3))
                    dve.tensor_tensor(xhat[:, :, :], xhat[:, :, :], shift[:, :].rearrange("p (o d) -> p o d", o=1).broadcast_to([128, NB, D]),
                                      ALU.add).then_inc(s["final_step"], 1)
                    dve.wait_ge(s["final_step"], value("last", g, pair, 2, 3))
                    dve.wait_ge(s["x1_loaded"], value("last", g, pair, 16, 16))
                    dve.tensor_tensor(xhat[:, :, :], xhat[:, :, :], rest_t[:, :].rearrange("p (k d) -> p k d", k=NB),
                                      ALU.add).then_inc(s["final_step"], 1)

            def body(g, pair):
                for n in range(SLOTS):
                    if has_max(g):
                        maximum(g, pair, 2 * n)
                    for use in chores(g, n):
                        chore(g, pair, use)
                    if n == AT_OUT and has_out(g):
                        region, free = filled(dve, g, pair, ("out", 0))
                        dve.scalar_tensor_tensor(node_t[:, :], flat(region), w_o[:, D:D + 1], res_sb[:, :],
                                                 ALU.mult, ALU.add).then_inc(free, 1)
                    if n == AT_RDEN and has_out(g):
                        dve.wait_ge(s["den_loaded"], value("out", g, pair, 16, 16))
                        dve.reciprocal(rden[:, :], den[:, :]).then_inc(s["rden_done"], 1)
                    if tail(g):
                        tail_part(g, pair, n)
                    if has_max(g):
                        maximum(g, pair, 2 * n + 1)

            def maximum(g, pair, u):
                region, free = filled(dve, g, pair, ("max", u))
                dve.tensor_reduce(mx[:, u // 32, u % 32 // 4, u % 4:u % 4 + 1], region, AX.XY, ALU.max).then_inc(free, 1)

            iterations(dve, body, G0 + 1)


_INS = ["L0_attn_x", "L0_attn_Wq", "L0_attn_bq", "L0_attn_Wk", "L0_attn_bk", "L0_attn_Wv", "L0_attn_bv", "L0_attn_Wo",
        "L0_attn_bo", "L0_ffn_ew", "L0_ffn_act_w", "L0_ffn_We", "L0_ffn_be", "L0_ffn_Wq", "L0_ffn_Wk", "L0_ffn_Wv",
        "L0_ffn_Wo", "L0_ffn_ln_g", "L0_ffn_ln_b"]


def kernel(**inputs):
    import numpy as np
    import concourse.bacc as bacc
    from concourse.bass_utils import run_bass_kernel_spmd

    nc = bacc.Bacc("TRN2", target_bir_lowering=False, num_devices=1)
    arrays, args = {}, []
    for name in _INS:
        a = np.ascontiguousarray(inputs[name])
        arrays[f"in_{name}"] = a
        args.append(nc.dram_tensor(f"in_{name}", a.shape, mybir.dt.from_np(a.dtype), kind="ExternalInput").ap())
    out = nc.dram_tensor("out", (B, S, D), F32, kind="ExternalOutput").ap()
    preln_attention_cell(nc, *args, out)
    r = run_bass_kernel_spmd(nc, [arrays], core_ids=[0])
    return r.results[0]["out"]
```
